# Optimizing a Trainium2 kernel written in Bass

```python
import numpy as np
import jax
import jax.numpy as jnp

def _softmax(x, axis=-1):
    return jax.nn.softmax(x, axis=axis)

def _gelu(x):
    return jax.nn.gelu(x, approximate=True)

def _silu(x):
    return jax.nn.silu(x)

def _sigmoid(x):
    return jax.nn.sigmoid(x)

def _layernorm(x, axis=-1, eps=1e-05):
    m = jnp.mean(x, axis=axis, keepdims=True)
    v = jnp.var(x, axis=axis, keepdims=True)
    return (x - m) / jnp.sqrt(v + eps)

def _scatter_add(tgt, idx, src, axis=0):
    return tgt.at[idx].add(src)

def _segment_sum(src, seg, n):
    return jax.ops.segment_sum(src, seg, n)
kernel_name = 'mk_macaron_d1_jaxref_r8_043eac'

def setup_inputs(seed: int=0):
    np.random.seed(seed)
    _w = jnp.asarray

    def _L0_attn_setup():
        import jax, jax.numpy as jnp
        import numpy as np
        from jax import lax
        N_EMBD = 128
        N_HEAD = 16
        HEAD_DIM = N_EMBD // N_HEAD
        EPS = 1e-06
        B, T = (4, 256)

        def _feature_map(x):
            return jax.nn.elu(x) + 1.0
        key = jax.random.key(seed)
        ks = jax.random.split(key, 5)
        scale = 1.0 / np.sqrt(N_EMBD)
        return {'x': jax.random.normal(ks[0], (B, T, N_EMBD), jnp.float32), 'W_attn': jax.random.normal(ks[1], (N_EMBD, 3 * N_EMBD), jnp.float32) * scale, 'b_attn': jax.random.normal(ks[2], (3 * N_EMBD,), jnp.float32) * 0.01, 'W_proj': jax.random.normal(ks[3], (N_EMBD, N_EMBD), jnp.float32) * scale, 'b_proj': jax.random.normal(ks[4], (N_EMBD,), jnp.float32) * 0.01}
    _L0_attn_in = _L0_attn_setup()

    def _L0_ffn_setup():
        import jax, jax.numpy as jnp
        import numpy as np
        B, S = (4, 64)
        H = 128
        I = 352
        E = 8
        K = 2
        IS = 176
        key = jax.random.key(seed)
        ks = jax.random.split(key, 8)

        def init(k, shape, fan_in):
            return (jax.random.normal(k, shape, jnp.float32) / np.sqrt(fan_in)).astype(jnp.float32)
        return {'hidden_states': jax.random.normal(ks[0], (B, S, H), jnp.float32), 'gate_w': init(ks[1], (H, E), H), 'Wg': init(ks[2], (E, H, I), H), 'Wu': init(ks[3], (E, H, I), H), 'Wd': init(ks[4], (E, I, H), I), 'Sg': init(ks[5], (H, IS), H), 'Su': init(ks[6], (H, IS), H), 'Sd': init(ks[7], (IS, H), IS)}
    _L0_ffn_in = _L0_ffn_setup()
    _d = {'L0_attn_x': _L0_attn_in['x'], 'L0_attn_W_attn': _L0_attn_in['W_attn'], 'L0_attn_b_attn': _L0_attn_in['b_attn'], 'L0_attn_W_proj': _L0_attn_in['W_proj'], 'L0_attn_b_proj': _L0_attn_in['b_proj'], 'L0_ffn_gate_w': _L0_ffn_in['gate_w'], 'L0_ffn_Wg': _L0_ffn_in['Wg'], 'L0_ffn_Wu': _L0_ffn_in['Wu'], 'L0_ffn_Wd': _L0_ffn_in['Wd'], 'L0_ffn_Sg': _L0_ffn_in['Sg'], 'L0_ffn_Su': _L0_ffn_in['Su'], 'L0_ffn_Sd': _L0_ffn_in['Sd']}
    _x0 = _d['L0_attn_x']
    _d['L0_attn_x'] = jax.random.normal(jax.random.fold_in(jax.random.key(seed), 1), (32, 256, 128), dtype=_x0.dtype)
    del _x0
    return _d

def reference(L0_attn_x, L0_attn_W_attn, L0_attn_b_attn, L0_attn_W_proj, L0_attn_b_proj, L0_ffn_gate_w, L0_ffn_Wg, L0_ffn_Wu, L0_ffn_Wd, L0_ffn_Sg, L0_ffn_Su, L0_ffn_Sd):

    def _L0_attn_ref(x, W_attn, b_attn, W_proj, b_proj):
        import jax, jax.numpy as jnp
        import numpy as np
        from jax import lax
        N_EMBD = 128
        N_HEAD = 16
        HEAD_DIM = N_EMBD // N_HEAD
        EPS = 1e-06
        B, T = (4, 256)

        def _feature_map(x):
            return jax.nn.elu(x) + 1.0
        Bb, Tt, C = x.shape
        qkv = x @ W_attn + b_attn
        q, k, v = jnp.split(qkv, 3, axis=-1)

        def to_heads(t):
            return t.reshape(Bb, Tt, N_HEAD, HEAD_DIM).transpose(1, 0, 2, 3)
        q = _feature_map(to_heads(q))
        k = _feature_map(to_heads(k))
        v = to_heads(v)

        def step(carry, inp):
            kv, ksum = carry
            qt, kt, vt = inp
            kv = kv + kt[..., :, None] * vt[..., None, :]
            ksum = ksum + kt
            num = jnp.einsum('bhi,bhij->bhj', qt, kv)
            den = jnp.einsum('bhi,bhi->bh', qt, ksum)[..., None] + EPS
            return ((kv, ksum), num / den)
        init = (jnp.zeros((Bb, N_HEAD, HEAD_DIM, HEAD_DIM), x.dtype), jnp.zeros((Bb, N_HEAD, HEAD_DIM), x.dtype))
        _, y = lax.scan(step, init, (q, k, v))
        y = y.transpose(1, 0, 2, 3).reshape(Bb, Tt, C)
        return y @ W_proj + b_proj

    def _L0_ffn_ref(hidden_states, gate_w, Wg, Wu, Wd, Sg, Su, Sd):
        import jax, jax.numpy as jnp
        import numpy as np
        B, S = (4, 64)
        H = 128
        I = 352
        E = 8
        K = 2
        IS = 176
        b, s, h = hidden_states.shape
        x = hidden_states.reshape(-1, h)
        T = x.shape[0]
        logits = x @ gate_w
        top_v, top_i = jax.lax.top_k(logits, K)
        top_p = jax.nn.softmax(top_v, axis=-1)
        combine = jnp.zeros((T, E), x.dtype).at[jnp.arange(T)[:, None], top_i].add(top_p)
        g = jnp.einsum('th,ehi->tei', x, Wg)
        u = jnp.einsum('th,ehi->tei', x, Wu)
        d = jnp.einsum('tei,eih->teh', jax.nn.silu(g) * u, Wd)
        expert_out = jnp.einsum('te,teh->th', combine, d)
        shared = jax.nn.silu(x @ Sg) * (x @ Su) @ Sd
        return (expert_out + shared).reshape(b, s, h)
    x = L0_attn_x
    x = x + 0.5 * _L0_ffn_ref(_layernorm(x, axis=-1), L0_ffn_gate_w, L0_ffn_Wg, L0_ffn_Wu, L0_ffn_Wd, L0_ffn_Sg, L0_ffn_Su, L0_ffn_Sd)
    x = x + _L0_attn_ref(_layernorm(x, axis=-1), L0_attn_W_attn, L0_attn_b_attn, L0_attn_W_proj, L0_attn_b_proj)
    x = x + 0.5 * _L0_ffn_ref(_layernorm(x, axis=-1), L0_ffn_gate_w, L0_ffn_Wg, L0_ffn_Wu, L0_ffn_Wd, L0_ffn_Sg, L0_ffn_Su, L0_ffn_Sd)
    return x

_drawn_inputs = setup_inputs


def setup_inputs(seed=0):
    import zlib

    import numpy as np

    out = dict(_drawn_inputs(seed))
    spreads = {}
    factors = {'L0_attn_b_attn': 3.526, 'L0_attn_b_proj': 3.795}
    for name, (base, spread) in spreads.items():
        noise = np.random.default_rng([zlib.crc32(name.encode()), seed]).standard_normal(out[name].shape)
        drawn = base * np.exp(spread * noise) if base else spread * noise
        out[name] = jnp.asarray(drawn.astype(out[name].dtype))
    for name, factor in factors.items():
        out[name] = (out[name] * factor).astype(out[name].dtype)
    return out
```

```python
from contextlib import ExitStack

import concourse.bass as bass
from concourse import mybir

F32, F16, I32, U32 = mybir.dt.float32, mybir.dt.float16, mybir.dt.int32, mybir.dt.uint32
ALU = mybir.AluOpType
ACT = mybir.ActivationFunctionType
AX = mybir.AxisListType

P = 128
D = 128
E = 8
K = 2
FI = 352
FS = 176
B, S = 32, 256
T = B * S
TILE = P
NJ = 4
GT = NJ * TILE
NG = T // GT
HEADS, HD = 16, 8
BLK = 256
HALVES = BLK // P
NBLK = T * K // BLK + E
NC = 3
FP = NC * P
SC = 2
SW = FS // SC
REGION = T + BLK
ROWS = E * REGION + E * BLK
WORDS = 130
NOTOK = float(1 << 20)

SX, SWT, SH, SY = 10, 8, 2, 4
EPS_LN, EPS_DEN = 1e-5, 1e-6
KVW = HEADS * HD * HD
PHASES = 5


def macaron(nc, x, w_attn, b_attn, w_proj, b_proj, gate_w, wg, wu, wd, sg, su, sd, out):
    ctx = ExitStack()
    with ctx:
        def sb(name, shape, dt=F32):
            return ctx.enter_context(nc.sbuf_tensor(name, shape, dt))

        def ps(name, shape, dt=F32):
            return ctx.enter_context(nc.psum_tensor(name, shape, dt))

        def sem(name):
            return ctx.enter_context(nc.semaphore(name))

        routed = nc.dram_tensor("routed_rows", (ROWS, WORDS), F32).ap()
        result = nc.dram_tensor("expert_results", (K * T, D), F32).ap()

        X = sb("X", [P, T // P * D])
        PR = sb("PR", [P, NG * NJ * K])
        WG = sb("WG", [P, 2, E * FP], F16)
        WU = sb("WU", [P, 2, E * FP], F16)
        WD = sb("WD", [P, 2, E * NC * D], F16)
        GW = sb("GW", [P, 2, E], F16)
        SGW = sb("SGW", [P, 2, FS], F16)
        SUW = sb("SUW", [P, 2, FS], F16)
        SDW = sb("SDW", [P, 2, SC * D], F16)
        AW = sb("AW", [P, 2, 3 * D], F16)
        PW = sb("PW", [P, 2, D], F16)
        stage = sb("stage", [P, E * NC * D])
        stage2 = sb("stage2", [P, 2 * FS + SC * D + 4 * D + E])
        bias_a = sb("bias_a", [P, 3 * D])
        bias_p = sb("bias_p", [P, D])
        ident = sb("ident", [P, P], F16)
        before = sb("before", [P, P], F16)
        ones16 = sb("ones16", [P, P], F16)
        upto = sb("upto", [P, P])
        ones32 = sb("ones32", [P, P])
        lower = sb("lower", [P, NJ, E, E])
        expert_no = sb("expert_no", [P, NJ, E])
        block_no = sb("block_no", [P, NBLK])
        base = sb("base", [P, E])
        base_i = sb("base_i", [P, E], I32)
        region0 = sb("region0", [P, E])
        pad_rows = sb("pad_rows", [P, HALVES, WORDS])
        xn = sb("xn", [P, 2, NJ * D])
        stats = sb("stats", [P, NJ, 6])
        newton = sb("newton", [P, 2, NJ])
        mv = [sb("mv_f", [P, NJ, 2]), sb("mv_a", [P, NJ, 2])]
        rstd = [sb("rstd_f", [P, NJ]), sb("rstd_a", [P, NJ])]
        row = [sb(f"row{u}", [P, NJ, WORDS]) for u in range(2)]
        xT = [sb(f"xT{u}", [P, 2, GT], F16) for u in range(2)]
        lg = sb("lg", [P, NJ, E])
        better = sb("better", [P, NJ, E, E])
        equal = sb("equal", [P, NJ, E, E])
        rank = sb("rank", [P, NJ, E])
        pick = sb("pick", [P, K, NJ, E])
        chosen = sb("chosen", [P, NJ, E], F16)
        posb = sb("posb", [P, NJ, E])
        pk = sb("pk", [P, K, NJ, E])
        vtop = sb("vtop", [P, K, NJ])
        th = sb("th", [P, NJ])
        dstf = [sb(f"dstf{u}", [P, K, NJ]) for u in range(2)]
        dstc = sb("dstc", [P, K, NJ])
        idx = [sb(f"idx{u}", [P, K, NJ], U32) for u in range(2)]
        ssil = sb("ssil", [SW, SC, GT])
        sh32 = sb("sh32", [SW, SC, GT])
        shT = sb("shT", [SW, 2, SC, GT], F16)
        nb = sb("nb", [P, E])
        nbi = sb("nbi", [P, E], I32)
        cum = sb("cum", [P, E])
        past = sb("past", [P, NBLK, E])
        eb = sb("eb", [P, NBLK])
        startb = sb("startb", [P, NBLK])
        rowf = sb("rowf", [P, NBLK])
        row_i = sb("row_i", [P, NBLK], I32)
        exp_i = sb("exp_i", [P, NBLK], I32)
        xe = [sb(f"xe{u}", [P, HALVES, WORDS]) for u in range(2)]
        eT = [sb(f"eT{u}", [P, 2, BLK], F16) for u in range(2)]
        esil = [sb(f"esil{u}", [P, NC * BLK]) for u in range(2)]
        eh32 = [sb(f"eh32{u}", [P, NC * BLK]) for u in range(2)]
        ehT = [sb(f"ehT{u}", [P, 2, NC, BLK], F16) for u in range(2)]
        ey = [sb(f"ey{u}", [P, HALVES, D]) for u in range(2)]
        second = sb("second", [P, HALVES])
        places = sb("places", [P, NBLK * HALVES], U32)
        eidx = [sb(f"eidx{u}", [P, HALVES], U32) for u in range(2)]
        Y = [sb(f"Y{u}", [P, K, NJ, D]) for u in range(2)]
        xa = sb("xa", [P, 2, NJ, D], F16)
        xaT = sb("xaT", [P, 2, GT], F16)
        qkv = sb("qkv", [P, 2, 3 * D])
        relu = sb("relu", [P, 2, 2 * D])
        kv = sb("kv", [P, 2, KVW])
        prod = sb("prod", [P, KVW])
        prodk = sb("prodk", [P, D])
        den = sb("den", [P, HEADS])
        rden = sb("rden", [P, HEADS])
        num = sb("num", [P, D])
        y32 = sb("y32", [P, NJ, D])
        ya = sb("ya", [P, 2, NJ, D], F16)
        yaT = sb("yaT", [P, 2, GT], F16)

        PSUM = ps("PSUM", [P, 8 * 512])

        def bank(n, m=1):
            return PSUM[:, 512 * n:512 * (n + m)]

        PT = bank(0).bitcast(F16)
        PL = bank(1)
        PG, PU = bank(2), bank(3)
        PO = bank(4)
        PKV = bank(5, 3)
        PE_T = bank(7).bitcast(F16)
        PE_Y = bank(6)

        s_load0, s_load1, s_x0, s_x1 = sem("s_load0"), sem("s_load1"), sem("s_x0"), sem("s_x1")
        s_const, s_const2, s_wprep, s_whi = sem("s_const"), sem("s_const2"), sem("s_wprep"), sem("s_whi")
        s_phase = sem("s_phase")
        s_xn, s_hi, s_lo, s_pt, s_xT = sem("s_xn"), sem("s_hi"), sem("s_lo"), sem("s_pt"), sem("s_xT")
        s_lg, s_chosen, s_pos, s_route = sem("s_lg"), sem("s_chosen"), sem("s_pos"), sem("s_route")
        s_vtop, s_th = sem("s_vtop"), sem("s_th")
        s_sgu, s_ssil, s_sh32, s_shhi, s_sh, s_so, s_sdone = (
            sem("s_sgu"), sem("s_ssil"), sem("s_sh32"), sem("s_shhi"), sem("s_sh"), sem("s_so"), sem("s_sdone"))
        s_scat = [sem("s_scat0"), sem("s_scat1")]
        s_base, s_pad, s_tab = sem("s_base"), sem("s_pad"), sem("s_tab")
        s_xe = [sem("s_xe0"), sem("s_xe1")]
        s_et, s_eT, s_egu, s_esil, s_eh32, s_ehi, s_eh, s_ey, s_eyb, s_eidx = (
            sem("s_et"), sem("s_eT"), sem("s_egu"), sem("s_esil"), sem("s_eh32"), sem("s_ehi"), sem("s_eh"),
            sem("s_ey"), sem("s_eyb"), sem("s_eidx"))
        s_res = [sem("s_res0"), sem("s_res1")]
        s_Y = [sem("s_Y0"), sem("s_Y1")]
        s_comb = sem("s_comb")
        s_axn, s_ahi, s_alo, s_at, s_aT = sem("s_axn"), sem("s_ahi"), sem("s_alo"), sem("s_at"), sem("s_aT")
        s_qkv, s_qkvb, s_ex, s_phi, s_kv, s_cum, s_cumu = (
            sem("s_qkv"), sem("s_qkvb"), sem("s_ex"), sem("s_phi"), sem("s_kv"), sem("s_cum"), sem("s_cumu"))
        s_y32, s_yhi, s_ylo, s_yt, s_yT, s_ao, s_adone = (
            sem("s_y32"), sem("s_yhi"), sem("s_ylo"), sem("s_yt"), sem("s_yT"), sem("s_ao"), sem("s_adone"))
        s_out = sem("s_out")

        def wait(eng, s, v):
            if not isinstance(v, int) or v > 0:
                eng.wait_ge(s, v)

        def phase_end(eng, n):
            eng.drain().then_inc(s_phase, 1)
            eng.wait_ge(s_phase, PHASES * n)

        def pairs(eng, first, last, step):
            step(first, 0)
            step(first + 1, 1)
            with eng.Fori(0, (last - first) // 2 - 2) as i:
                step(i * 2 + (first + 2), 0)
                step(i * 2 + (first + 3), 1)
            step(last - 2, 0)
            step(last - 1, 1)

        def cols(n, width, at=0, size=None):
            return bass.ds(n * width + at, width if size is None else size)

        def X3(n):
            return X[:, cols(n, GT)].rearrange("p (j d) -> p j d", j=NJ)

        block = ctx.enter_context(nc.Block())

        @block.sync
        def _(sp):
            o = 0
            for w, n in ((gate_w, E), (sg, FS), (su, FS), (w_attn, 3 * D), (w_proj, D)):
                sp.dma_start(stage2[:, o:o + n], w).then_inc(s_load0, 16)
                o += n
            for c in range(SC):
                sp.dma_start(stage2[0:SW, o:o + D], sd[c * SW:(c + 1) * SW, :]).then_inc(s_load0, 16)
                o += D
            sp.dma_start(bias_a[:, :], b_attn.rearrange("(a n) -> a n", a=1).to_broadcast([P, 3 * D])).then_inc(s_load0, 16)
            sp.dma_start(bias_p[:, :], b_proj.rearrange("(a n) -> a n", a=1).to_broadcast([P, D])).then_inc(s_load0, 16)

            def tokens(ap, g):
                return ap[g * GT:(g + 1) * GT, :].rearrange("(j p) d -> p j d", p=P)

            for g in range(NG):
                sp.dma_start(X3(g), tokens(x, g)).then_inc(s_x0 if g < 2 else s_x1, 16)

            def load_expert(w, n, width):
                wait(sp, s_wprep, n + 1 if n else 0)
                if width is not None:
                    sp.dma_start(stage[:, 0:E * FI].rearrange("p (e i) -> p e i", e=E),
                                 w.rearrange("e h i -> h e i")).then_inc(s_load1, 16)
                else:
                    v = stage[:, :].rearrange("p (e c h) -> p e c h", e=E, c=NC)
                    for c in range(NC):
                        k = min(P, FI - c * P)
                        sp.dma_start(v[0:k, :, c, :], w[:, c * P:c * P + k, :].rearrange("e k h -> k e h")
                                     ).then_inc(s_load1, 16)

            load_expert(wg, 0, FI)
            load_expert(wu, 1, FI)
            load_expert(wd, 2, None)

            def pads(f):
                wait(sp, s_base, f + 1)
                for e in range(E):
                    at = sp.value_load(base_i[0:1, e:e + 1], min_val=e * REGION, max_val=e * REGION + T)
                    sp.dma_start(routed[bass.ds(at, BLK), :].rearrange("(h p) w -> p h w", p=P),
                                 pad_rows[:, :, :]).then_inc(s_pad, 16)
                sp.wait_ge(s_pad, 16 * (E * (f + 2)))

            def load_block(f):
                def step(n, u):
                    m = n - f * NBLK
                    wait(sp, s_eT, n - 1)
                    at = sp.value_load(row_i[0:1, bass.ds(m, 1)], min_val=0, max_val=ROWS - BLK)
                    sp.dma_start(xe[u][:, :, :], routed[bass.ds(at, BLK), :].rearrange("(h p) w -> p h w", p=P)
                                 ).then_inc(s_xe[u], 16)
                return step

            def load_results(n, u):
                wait(sp, s_comb, n - 1)
                for k in range(K):
                    g = n % NG if isinstance(n, int) else n - n_off[0]
                    sp.dma_start(Y[u][:, k, :, :],
                                 result[bass.ds(g * GT + k * T, GT), :].rearrange("(j p) d -> p j d", p=P)
                                 ).then_inc(s_Y[u], 16)

            sp.wait_ge(s_const, 1)
            for e in range(E):
                sp.dma_start(routed[E * REGION + e * BLK:E * REGION + (e + 1) * BLK, :].rearrange("(h p) w -> p h w", p=P),
                             pad_rows[:, :, :]).then_inc(s_pad, 16)
            n_off = [0]
            for f in range(2):
                pads(f)
                phase_end(sp, 2 * f + 1)
                pairs(sp, f * NBLK, (f + 1) * NBLK, load_block(f))
                phase_end(sp, 2 * f + 2)
                n_off[0] = f * NG
                if f == 0:
                    pairs(sp, 0, NG, load_results)

            def last(n, u):
                load_results(n, u)

            outT = out
            def store(n, u):
                g = n - NG
                sp.wait_ge(s_comb, n + 1)
                sp.dma_start(outT[bass.ds(g * GT, GT), :].rearrange("(j p) d -> p j d", p=P), X3(g)).then_inc(s_out, 16)

            load_results_step = load_results
            load_results_step(NG, 0)
            load_results_step(NG + 1, 1)
            with sp.Fori(0, NG // 2 - 1) as i:
                for u in range(2):
                    store(i * 2 + (NG + u), u)
                    load_results_step(i * 2 + (NG + 2 + u), u)
            for u in range(2):
                store(2 * NG - 2 + u, u)
            sp.wait_ge(s_out, 16 * NG)

        @block.gpsimd
        def _(pool):
            pool.memset(ones16[:, :], 1.0)
            pool.memset(ones32[:, :], 1.0)
            pool.memset(ident[:, :], 0.0)
            pool.memset(lower[:, :, :, :], 1.0)
            pool.memset(pad_rows[:, :, :], 0.0)
            pool.drain()
            pool.memset(pad_rows[:, :, WORDS - 2:WORDS - 1], NOTOK)
            pool.drain().then_inc(s_const, 1)
            pool.affine_select(out=ident[:, :], in_=ident[:, :], compare_op=ALU.not_equal, fill=1.0, base=0,
                               pattern=[[-1, P]], channel_multiplier=1)
            pool.affine_select(out=before[:, :], in_=ones16[:, :], compare_op=ALU.is_gt, fill=0.0, base=0,
                               pattern=[[1, P]], channel_multiplier=-1)
            pool.affine_select(out=upto[:, :], in_=ones32[:, :], compare_op=ALU.is_ge, fill=0.0, base=0,
                               pattern=[[1, P]], channel_multiplier=-1)
            pool.affine_select(out=lower[:, :, :, :], in_=lower[:, :, :, :], compare_op=ALU.is_gt, fill=0.0, base=0,
                               pattern=[[0, NJ], [1, E], [-1, E]], channel_multiplier=0)
            pool.iota(expert_no[:, :, :], [[0, NJ], [1, E]], base=0, channel_multiplier=0,
                      allow_small_or_imprecise_dtypes=True)
            pool.iota(block_no[:, :], [[1, NBLK]], base=0, channel_multiplier=0,
                      allow_small_or_imprecise_dtypes=True)
            pool.iota(region0[:, :], [[REGION, E]], base=0, channel_multiplier=0,
                      allow_small_or_imprecise_dtypes=True)
            for u in range(2):
                pool.iota(row[u][:, :, WORDS - 2], [[TILE, NJ]], base=u * GT, channel_multiplier=1,
                          allow_small_or_imprecise_dtypes=True)
            pool.drain().then_inc(s_const2, 1)

            def scatter(n, u):
                pool.wait_ge(s_route, n + 1)
                pool.tensor_tensor(dstc[:, :, :], dstf[u][:, :, :],
                                   ones32[:, 0:K * NJ].rearrange("p (k j) -> p k j", k=K), ALU.mult)
                pool.drain()
                pool.tensor_copy(idx[u][:, :, :], dstc[:, :, :])
                pool.drain()
                for k in range(K):
                    for j in range(NJ):
                        pool.indirect_dma_start(routed, bass.IndirectOffsetOnAxis(ap=idx[u][:, k, j:j + 1], axis=0),
                                                row[u][:, j, :], None).then_inc(s_scat[u], 16)

            def results(n, u):
                wait(pool, s_res[u], (n - u) * (16 * HALVES // 2))
                pool.wait_ge(s_eyb, n + 1)
                pool.tensor_copy(eidx[u][:, :], places[:, cols(n - f_now[0] * NBLK, HALVES)])
                pool.drain()
                for h in range(HALVES):
                    pool.indirect_dma_start(result, bass.IndirectOffsetOnAxis(ap=eidx[u][:, h:h + 1], axis=0),
                                            ey[u][:, h, :], None, bounds_check=K * T - 1, oob_is_err=False
                                            ).then_inc(s_res[u], 16)

            def outer(n2):
                pool.wait_ge(s_phi, n2 + 1)
                for a in range(2):
                    k4 = qkv[:, a, D:2 * D].rearrange("p (h i j) -> p h i j", h=HEADS, j=1).to_broadcast([P, HEADS, HD, HD])
                    v4 = qkv[:, a, 2 * D:3 * D].rearrange("p (h i j) -> p h i j", h=HEADS, i=1).to_broadcast([P, HEADS, HD, HD])
                    last = pool.tensor_tensor(kv[:, a, :].rearrange("p (h i j) -> p h i j", h=HEADS, i=HD), k4, v4, ALU.mult)
                last.then_inc(s_kv, 1)

            f_now = [0]
            for f in range(2):
                f_now[0] = f
                if f == 0:
                    pairs(pool, 0, NG, scatter)
                else:
                    def both(n, u):
                        outer(n * 2 - 2 * NG)
                        outer(n * 2 - (2 * NG - 1))
                        scatter(n, u)
                    pairs(pool, NG, 2 * NG, both)
                for u in range(2):
                    pool.wait_ge(s_scat[u], 16 * K * NJ * NG // 2 * (f + 1))
                phase_end(pool, 2 * f + 1)
                pairs(pool, f * NBLK, (f + 1) * NBLK, results)
                for u in range(2):
                    pool.wait_ge(s_res[u], 16 * HALVES * NBLK // 2 * (f + 1))
                phase_end(pool, 2 * f + 2)

        @block.scalar
        def _(act):
            def part(dst, src):
                act.activation(dst, src, ACT.Copy, scale=float(2 ** SWT))

            act.wait_ge(s_load0, 16 * 9)
            act.wait_ge(s_wprep, 1)
            o = 0
            for w, n in ((GW, E), (SGW, FS), (SUW, FS), (AW, 3 * D), (PW, D)):
                part(w[:, 0, :], stage2[:, o:o + n])
                o += n
            part(SDW[0:SW, 0, :], stage2[0:SW, o:o + SC * D])
            act.drain().then_inc(s_whi, 1)

            act.wait_ge(s_load1, 16)
            part(WG[:, 0, :].rearrange("p (e i) -> p e i", e=E)[:, :, 0:FI], stage[:, 0:E * FI].rearrange("p (e i) -> p e i", e=E))
            act.drain().then_inc(s_whi, 1)
            act.wait_ge(s_load1, 32)
            part(WU[:, 0, :].rearrange("p (e i) -> p e i", e=E)[:, :, 0:FI], stage[:, 0:E * FI].rearrange("p (e i) -> p e i", e=E))
            act.drain().then_inc(s_whi, 1)
            act.wait_ge(s_load1, 16 * 5)
            v, w = stage[:, :].rearrange("p (e c h) -> p e c h", e=E, c=NC), WD[:, 0, :].rearrange("p (e c h) -> p e c h", e=E, c=NC)
            part(w[:, :, 0:NC - 1, :], v[:, :, 0:NC - 1, :])
            part(w[0:FI - 2 * P, :, NC - 1, :], v[0:FI - 2 * P, :, NC - 1, :])
            act.drain().then_inc(s_whi, 1)

            def high(n, u):
                act.wait_ge(s_xn, n + 1)
                act.activation(row[u][:, :, 0:D // 2].bitcast(F16), xn[:, 0, :].rearrange("p (j d) -> p j d", j=NJ),
                               ACT.Copy, scale=float(2 ** SX)).then_inc(s_hi, 1)

            def evacuate(n, u):
                act.wait_ge(s_pt, n + 1)
                act.activation(xT[u][:, :, :], PT[:, :].rearrange("p (a t) -> p a t", a=2), ACT.Copy).then_inc(s_xT, 1)

            def shared(n):
                for c in range(SC):
                    act.wait_ge(s_sgu, n * SC + (c + 1))
                    if c == 0:
                        wait(act, s_sh, n)
                    act.activation(ssil[:, c, :], PG[0:SW, :], ACT.Silu, scale=2.0 ** -(SX + SWT)).then_inc(s_ssil, 1)
                act.wait_ge(s_sh32, n * SC + SC)
                wait(act, s_so, n)
                act.activation(shT[:, 0, :, :], sh32[:, :, :], ACT.Copy).then_inc(s_shhi, 1)

            def tanh(n):
                act.wait_ge(s_vtop, n + 1)
                act.activation(th[:, :], vtop[:, 0, :], ACT.Tanh, scale=0.5 * 2.0 ** -(SX + SWT)).then_inc(s_th, 1)

            def route(n, u):
                high(n, u)
                evacuate(n, u)
                tanh(n)
                shared(n)

            def attention(m):
                act.wait_ge(s_axn, m + 1)
                act.activation(xa[:, 0, :, :], xn[:, 1, :].rearrange("p (j d) -> p j d", j=NJ),
                               ACT.Copy, scale=float(2 ** SX)).then_inc(s_ahi, 1)
                act.wait_ge(s_at, m + 1)
                act.activation(xaT[:, :, :], PT[:, :].rearrange("p (a t) -> p a t", a=2), ACT.Copy).then_inc(s_aT, 1)
                for q in range(2):
                    act.wait_ge(s_qkvb, m * 2 + (q + 1))
                    act.activation(relu[:, :, :], qkv[:, :, 0:2 * D], ACT.Relu, scale=-1.0)
                    act.drain()
                    act.activation(relu[:, :, :], relu[:, :, :], ACT.Exp, scale=-1.0).then_inc(s_ex, 1)
                act.wait_ge(s_y32, m + 1)
                act.activation(ya[:, 0, :, :], y32[:, :, :], ACT.Copy, scale=float(2 ** SY)).then_inc(s_yhi, 1)
                act.wait_ge(s_yt, m + 1)
                act.activation(yaT[:, :, :], PT[:, :].rearrange("p (a t) -> p a t", a=2), ACT.Copy).then_inc(s_yT, 1)

            def silu(n, u):
                act.wait_ge(s_egu, n + 1)
                act.activation(esil[u][:, :], PSUM[:, 1536 * u:1536 * u + 768], ACT.Silu,
                               scale=2.0 ** -(SX + SWT)).then_inc(s_esil, 1)

            def hi(n, u):
                act.wait_ge(s_eh32, n + 1)
                act.activation(ehT[u][:, 0, :, :], eh32[u][:, :].rearrange("p (c t) -> p c t", c=NC), ACT.Copy
                               ).then_inc(s_ehi, 1)

            def results(n, u):
                act.wait_ge(s_ey, n + 1)
                wait(act, s_res[u], res_value(n, u))
                act.activation(ey[u][:, :, :], PE_Y[:, 0:BLK].rearrange("p (h d) -> p h d", h=HALVES), ACT.Copy,
                               scale=0.5 * 2.0 ** -(SH + SWT)).then_inc(s_eyb, 1)

            def res_value(n, u):
                return (n - u) * (16 * HALVES // 2)

            def experts(f):
                n0, n1 = f * NBLK, (f + 1) * NBLK

                def step(n, u):
                    silu(n, u)
                    hi(n - 1, 1 - u)
                    results(n - 2, u)

                silu(n0, 0)
                silu(n0 + 1, 1)
                hi(n0, 0)
                with act.Fori(0, (NBLK - 2) // 2) as i:
                    step(i * 2 + (n0 + 2), 0)
                    step(i * 2 + (n0 + 3), 1)
                hi(n1 - 1, 1)
                results(n1 - 2, 0)
                results(n1 - 1, 1)

            pairs(act, 0, NG, route)
            phase_end(act, 1)
            experts(0)
            phase_end(act, 2)

            def both(n, u):
                attention(n - NG)
                route(n, u)

            pairs(act, NG, 2 * NG, both)
            phase_end(act, 3)
            experts(1)
            phase_end(act, 4)

        @block.tensor
        def _(pe):
            def product(dst, a, b, start=True, stop=True):
                pe.matmul(dst, a[0], b[0], start=start, stop=False)
                pe.matmul(dst, a[0], b[1], start=False, stop=False)
                return pe.matmul(dst, a[1], b[0], start=False, stop=stop)

            def transpose_group(src, s):
                for part in range(2):
                    for j in range(NJ):
                        mm = pe.transpose(PT[:, part * GT + j * P:part * GT + (j + 1) * P], src(part, j), ident[:, :])
                mm.then_inc(s, 1)

            def transposes(n, u):
                pe.wait_ge(s_lo, n + 1)
                wait(pe, s_xT, n)
                if not isinstance(n, int) or n > NG:
                    pass
                transpose_group(lambda part, j: row[u][:, j, part * D // 2:(part + 1) * D // 2].bitcast(F16), s_pt)

            def logits(n, u):
                pe.wait_ge(s_xT, n + 1)
                for j in range(NJ):
                    t = slice(j * P, (j + 1) * P)
                    for a, b in ((0, 0), (0, 1), (1, 0), (1, 1)):
                        mm = pe.matmul(PL[:, j * E:(j + 1) * E], xT[u][:, a, t], GW[:, b, :], start=(a + b == 0), stop=(a + b == 2))
                mm.then_inc(s_lg, 1)

            def gate_up(n, u):
                for c in range(SC):
                    w = slice(c * SW, (c + 1) * SW)
                    wait(pe, s_sh32, n * SC + c)
                    product(PG[0:SW, :], [SGW[:, 0, w], SGW[:, 1, w]], [xT[u][:, 0, :], xT[u][:, 1, :]])
                    product(PU[0:SW, :], [SUW[:, 0, w], SUW[:, 1, w]], [xT[u][:, 0, :], xT[u][:, 1, :]]).then_inc(s_sgu, 1)

            def positions(n):
                pe.wait_ge(s_chosen, n + 1)
                pos = PL[:, 64:64 + (NJ + 1) * E]
                ch = chosen[:, :, :].rearrange("p j e -> p (j e)")
                pe.matmul(pos[:, 0:NJ * E], before[:, :], ch, start=True, stop=False, skip_group_check=True)
                for d in range(1, NJ + 1):
                    mm = pe.matmul(pos[:, d * E:(NJ + 1) * E], ones16[:, :], ch[:, 0:(NJ + 1 - d) * E], start=False,
                                   stop=(d == NJ), skip_group_check=True)
                mm.then_inc(s_pos, 1)

            def down(n):
                pe.wait_ge(s_sh, n + 1)
                wait(pe, s_sdone, n)
                for j in range(NJ):
                    t = slice(j * P, (j + 1) * P)
                    for c in range(SC):
                        h = slice(c * D, (c + 1) * D)
                        mm = product(PO[:, j * D:(j + 1) * D], [shT[:, 0, c, t], shT[:, 1, c, t]],
                                     [SDW[0:SW, 0, h], SDW[0:SW, 1, h]], start=(c == 0), stop=(c == SC - 1))
                mm.then_inc(s_so, 1)

            def route(n, u):
                transposes(n, u)
                logits(n, u)
                gate_up(n, u)
                positions(n)
                down(n)

            def attention(m):
                pe.wait_ge(s_alo, m + 1)
                transpose_group(lambda part, j: xa[:, part, j, :], s_at)
                pe.wait_ge(s_aT, m + 1)
                for q in range(2):
                    wait(pe, s_qkvb, m * 2 + q)
                    for a in range(2):
                        t = slice((2 * q + a) * P, (2 * q + a + 1) * P)
                        mm = product([PG, PU][a][:, 0:3 * D], [xaT[:, 0, t], xaT[:, 1, t]], [AW[:, 0, :], AW[:, 1, :]])
                    mm.then_inc(s_qkv, 1)
                    pe.wait_ge(s_kv, m * 2 + (q + 1))
                    for a in range(2):
                        wait(pe, s_cumu, m * 4 + 2 * q + a)
                        for lo, hi, src in ((0, 512, kv), (512, 1024, kv), (1024, 1024 + D, None)):
                            def cols_of(b):
                                return kv[:, b, lo:hi] if src is not None else qkv[:, b, D:2 * D]
                            mm = pe.matmul(PKV[:, lo:hi], upto[:, :], cols_of(a), start=True, stop=(a == 0))
                            if a:
                                mm = pe.matmul(PKV[:, lo:hi], ones32[:, :], cols_of(0), start=False, stop=True)
                        mm.then_inc(s_cum, 1)
                pe.wait_ge(s_ylo, m + 1)
                transpose_group(lambda part, j: ya[:, part, j, :], s_yt)
                pe.wait_ge(s_yT, m + 1)
                for j in range(NJ):
                    t = slice(j * P, (j + 1) * P)
                    mm = product(PO[:, j * D:(j + 1) * D], [yaT[:, 0, t], yaT[:, 1, t]], [PW[:, 0, :], PW[:, 1, :]])
                mm.then_inc(s_ao, 1)

            def block_transposes(n, u):
                pe.wait_ge(s_xe[u], (n - u) * 8 + 16)
                wait(pe, s_eT, n)
                for part in range(2):
                    for h in range(HALVES):
                        at = part * BLK + h * P
                        mm = pe.transpose(PE_T[:, at:at + P],
                                          xe[u][:, h, part * D // 2:(part + 1) * D // 2].bitcast(F16), ident[:, :])
                mm.then_inc(s_et, 1)

            def block_gate_up(n, u, m):
                e = pe.value_load(exp_i[0:1, bass.ds(m, 1)], min_val=0, max_val=E - 1)
                pe.wait_ge(s_eT, n + 1)
                wait(pe, s_eh32, n - 1)
                for W, o in ((WG, 0), (WU, NC * BLK)):
                    for c in range(NC):
                        w = [W[:, a, bass.ds(e * FP + c * P, P)] for a in range(2)]
                        at = 1536 * u + o + c * BLK
                        mm = product(PSUM[:, at:at + BLK], w, [eT[u][:, 0, :], eT[u][:, 1, :]])
                mm.then_inc(s_egu, 1)

            def block_down(n, u, m):
                e = pe.value_load(exp_i[0:1, bass.ds(m, 1)], min_val=0, max_val=E - 1)
                pe.wait_ge(s_eh, n + 1)
                wait(pe, s_eyb, n)
                for h in range(HALVES):
                    t = slice(h * P, (h + 1) * P)
                    for c in range(NC):
                        w = [WD[:, a, bass.ds(e * (NC * D) + c * D, D)] for a in range(2)]
                        mm = product(PE_Y[:, h * D:(h + 1) * D], [ehT[u][:, 0, c, t], ehT[u][:, 1, c, t]], w,
                                     start=(c == 0), stop=(c == NC - 1))
                mm.then_inc(s_ey, 1)

            def experts(f):
                n0, n1 = f * NBLK, (f + 1) * NBLK

                def step(n, u, down=True, ahead=True):
                    block_gate_up(n, u, n - n0)
                    if ahead:
                        block_transposes(n + 1, 1 - u)
                    if down:
                        block_down(n - 2, u, n - n0 - 2)

                block_transposes(n0, 0)
                step(n0, 0, down=False)
                step(n0 + 1, 1, down=False)
                with pe.Fori(0, (NBLK - 4) // 2) as i:
                    step(i * 2 + (n0 + 2), 0)
                    step(i * 2 + (n0 + 3), 1)
                step(n1 - 2, 0)
                step(n1 - 1, 1, ahead=False)
                block_down(n1 - 2, 0, NBLK - 2)
                block_down(n1 - 1, 1, NBLK - 1)

            pe.wait_ge(s_const2, 1)
            pe.wait_ge(s_wprep, 4)
            pairs(pe, 0, NG, route)
            phase_end(pe, 1)
            experts(0)
            phase_end(pe, 2)

            def both(n, u):
                attention(n - NG)
                route(n, u)

            pairs(pe, NG, 2 * NG, both)
            phase_end(pe, 3)
            experts(1)
            phase_end(pe, 4)

        @block.vector
        def _(dve):
            def low(dst, src, high, scale):
                return dve.scalar_tensor_tensor(out=dst, in0=src, scalar=float(2 ** scale), in1=high,
                                                op0=ALU.mult, op1=ALU.subtract)

            def e3(ap, n):
                return ap.rearrange("p (e i) -> p e i", e=E)[:, :, 0:n]

            for W in (WG, WU, WD):
                dve.memset(W[:, :, :].bitcast(F32), 0.0)
            dve.drain().then_inc(s_wprep, 1)

            dve.wait_ge(s_whi, 1)
            o = 0
            for w, n in ((GW, E), (SGW, FS), (SUW, FS), (AW, 3 * D), (PW, D)):
                low(w[:, 1, :], stage2[:, o:o + n], w[:, 0, :], SWT)
                o += n
            low(SDW[0:SW, 1, :], stage2[0:SW, o:o + SC * D], SDW[0:SW, 0, :], SWT)
            for n, W in ((2, WG), (3, WU)):
                dve.wait_ge(s_whi, n)
                low(e3(W[:, 1, :], FI), stage[:, 0:E * FI].rearrange("p (e i) -> p e i", e=E), e3(W[:, 0, :], FI), SWT)
                dve.drain().then_inc(s_wprep, 1)
            dve.wait_ge(s_whi, 4)
            v = stage[:, :].rearrange("p (e c h) -> p e c h", e=E, c=NC)
            w = [WD[:, a, :].rearrange("p (e c h) -> p e c h", e=E, c=NC) for a in range(2)]
            low(w[1][:, :, 0:NC - 1, :], v[:, :, 0:NC - 1, :], w[0][:, :, 0:NC - 1, :], SWT)
            q = FI - 2 * P
            low(w[1][0:q, :, NC - 1, :], v[0:q, :, NC - 1, :], w[0][0:q, :, NC - 1, :], SWT)
            dve.drain().then_inc(s_wprep, 1)

            def statistics(which, g):
                xs = X3(g)
                for j in range(NJ):
                    dve.bn_stats(stats[:, j, :], xs[:, j, :])
                dve.drain()
                for j in range(NJ):
                    dve.bn_aggr(mv[which][:, j, :], stats[:, j, :])
                dve.drain()
                v, y, a = newton[:, 0, :], rstd[which][:, :], newton[:, 1, :]
                dve.tensor_scalar(v, mv[which][:, :, 1], EPS_LN, None, ALU.add)
                dve.drain()
                dve.tensor_single_scalar(a.bitcast(I32), v.bitcast(I32), 1, ALU.arith_shift_right)
                dve.drain()
                dve.tensor_scalar(y.bitcast(I32), a.bitcast(I32), -1.0, float(0x5f3759df), ALU.mult, ALU.add)
                dve.drain()
                for _ in range(3):
                    dve.tensor_tensor(a, y, y, ALU.mult)
                    dve.drain()
                    dve.scalar_tensor_tensor(out=a, in0=a, scalar=-0.5, in1=v, op0=ALU.mult, op1=ALU.mult)
                    dve.drain()
                    dve.scalar_tensor_tensor(out=y, in0=a, scalar=1.5, in1=y, op0=ALU.add, op1=ALU.mult)
                    dve.drain()

            def normalize(which, n, g, dst):
                xs = X3(g)
                for j in range(NJ):
                    last = dve.tensor_scalar(dst[:, j * D:(j + 1) * D], xs[:, j, :], mv[which][:, j, 0:1],
                                             rstd[which][:, j:j + 1], ALU.subtract, ALU.mult)
                return last

            def normed(n, u, g):
                wait(dve, s_scat[u], (n - u) * (16 * K * NJ // 2))
                normalize(0, n, g, xn[:, 0, :]).then_inc(s_xn, 1)
                dve.wait_ge(s_hi, n + 1)
                low(row[u][:, :, D // 2:D].bitcast(F16), xn[:, 0, :].rearrange("p (j d) -> p j d", j=NJ),
                    row[u][:, :, 0:D // 2].bitcast(F16), SX).then_inc(s_lo, 1)

            def choose(n, u, g):
                dve.wait_ge(s_lg, n + 1)
                dve.tensor_copy(lg[:, :, :], PL[:, 0:NJ * E].rearrange("p (j e) -> p j e", j=NJ))
                dve.drain()
                mine = lg[:, :, :].rearrange("p j (e f) -> p j e f", f=1).to_broadcast([P, NJ, E, E])
                theirs = lg[:, :, :].rearrange("p j (f e) -> p j f e", f=1).to_broadcast([P, NJ, E, E])
                dve.tensor_tensor(better[:, :, :, :], theirs, mine, ALU.is_gt)
                dve.tensor_tensor(equal[:, :, :, :], theirs, mine, ALU.is_equal)
                dve.drain()
                dve.tensor_tensor(equal[:, :, :, :], equal[:, :, :, :], lower[:, :, :, :], ALU.mult)
                dve.drain()
                dve.tensor_tensor(better[:, :, :, :], better[:, :, :, :], equal[:, :, :, :], ALU.add)
                dve.drain()
                dve.tensor_reduce(rank[:, :, :], better[:, :, :, :], AX.X, ALU.add)
                dve.drain()
                dve.tensor_scalar(chosen[:, :, :], rank[:, :, :], float(K), None, ALU.is_lt).then_inc(s_chosen, 1)
                for k in range(K):
                    dve.tensor_scalar(pick[:, k, :, :], rank[:, :, :], float(k), None, ALU.is_equal)
                dve.drain()
                lk = lg[:, :, :].rearrange("p (k j) e -> p k j e", k=1).to_broadcast([P, K, NJ, E])
                dve.tensor_tensor(pk[:, :, :, :], pick[:, :, :, :], lk, ALU.mult)
                dve.tensor_tensor(posb[:, :, :], pick[:, 0, :, :], expert_no[:, :, :], ALU.mult)
                dve.drain()
                dve.tensor_reduce(vtop[:, :, :], pk[:, :, :, :], AX.X, ALU.add)
                dve.tensor_reduce(row[u][:, :, WORDS - 1], posb[:, :, :], AX.X, ALU.add)
                if not isinstance(n, int) or n % NG >= 2:
                    dve.tensor_scalar(row[u][:, :, WORDS - 2], row[u][:, :, WORDS - 2], float(2 * GT), None, ALU.add)
                elif n >= NG:
                    dve.tensor_scalar(row[u][:, :, WORDS - 2], row[u][:, :, WORDS - 2], float(2 * GT - T), None, ALU.add)
                dve.drain()
                dve.tensor_tensor(vtop[:, 0, :], vtop[:, 0, :], vtop[:, 1, :], ALU.subtract).then_inc(s_vtop, 1)

            def place(n, u, g):
                dve.wait_ge(s_pos, n + 1)
                pos = PL[:, 64:64 + (NJ + 1) * E].rearrange("p (j e) -> p j e", j=NJ + 1)
                bj = base[:, :].rearrange("p (j e) -> p j e", j=1).to_broadcast([P, NJ, E])
                dve.tensor_tensor(posb[:, :, :], pos[:, 0:NJ, :], bj, ALU.add)
                dve.drain()
                dve.tensor_tensor(base[:, :], base[:, :], pos[:, NJ, :], ALU.add)
                pb = posb[:, :, :].rearrange("p (k j) e -> p k j e", k=1).to_broadcast([P, K, NJ, E])
                dve.tensor_tensor(pk[:, :, :, :], pick[:, :, :, :], pb, ALU.mult)
                dve.drain()
                dve.tensor_reduce(dstf[u][:, :, :], pk[:, :, :, :], AX.X, ALU.add).then_inc(s_route, 1)
                dve.wait_ge(s_th, n + 1)
                pr = PR[:, cols(g, NJ * K)].rearrange("p (j k) -> p j k", k=K)
                for k in range(K):
                    dve.tensor_scalar(pr[:, :, k], th[:, :], 0.5 - k, 0.5, ALU.mult, ALU.add)

            def shared(n, g):
                for c in range(SC):
                    dve.wait_ge(s_ssil, n * SC + (c + 1))
                    dve.scalar_tensor_tensor(out=sh32[:, c, :], in0=PU[0:SW, :], scalar=2.0 ** (SH - SX - SWT),
                                             in1=ssil[:, c, :], op0=ALU.mult, op1=ALU.mult).then_inc(s_sh32, 1)

            def shared_low(n):
                dve.wait_ge(s_shhi, n + 1)
                low(shT[:, 1, :, :], sh32[:, :, :], shT[:, 0, :, :], 0).then_inc(s_sh, 1)

            def shared_add(n, g):
                dve.wait_ge(s_so, n + 1)
                xg = X[:, cols(g, GT)]
                dve.scalar_tensor_tensor(out=xg, in0=PO[:, :], scalar=0.5 * 2.0 ** -(SH + SWT), in1=xg,
                                         op0=ALU.mult, op1=ALU.add).then_inc(s_sdone, 1)

            def route(n, u, g, ahead):
                normed(n, u, g)
                choose(n, u, g)
                shared(n, g)
                ahead()
                place(n, u, g)
                shared_low(n)
                shared_add(n, g)

            def tables(f):
                dve.drain()
                dve.tensor_copy(base_i[:, :], base[:, :]).then_inc(s_base, 1)
                dve.tensor_tensor(nb[:, :], base[:, :], region0[:, :], ALU.subtract)
                dve.drain()
                dve.tensor_scalar(nb[:, :], nb[:, :], float(BLK - 1), None, ALU.add)
                dve.drain()
                dve.tensor_copy(nbi[:, :], nb[:, :])
                dve.drain()
                dve.tensor_single_scalar(nbi[:, :], nbi[:, :], BLK.bit_length() - 1, ALU.arith_shift_right)
                dve.drain()
                dve.tensor_copy(nb[:, :], nbi[:, :])
                dve.drain()
                dve.tensor_copy(cum[:, 0:1], nb[:, 0:1])
                for e in range(1, E):
                    dve.drain()
                    dve.tensor_tensor(cum[:, e:e + 1], cum[:, e - 1:e], nb[:, e:e + 1], ALU.add)
                dve.drain()
                dve.tensor_tensor(past[:, :, :], block_no[:, :].rearrange("p (b e) -> p b e", e=1).to_broadcast([P, NBLK, E]),
                                  cum[:, :].rearrange("p (b e) -> p b e", b=1).to_broadcast([P, NBLK, E]), ALU.is_ge)
                dve.drain()
                dve.tensor_reduce(eb[:, :], past[:, :, :], AX.X, ALU.add)
                dve.drain()
                dve.tensor_tensor(past[:, :, :], past[:, :, :],
                                  nb[:, :].rearrange("p (b e) -> p b e", b=1).to_broadcast([P, NBLK, E]), ALU.mult)
                dve.drain()
                dve.tensor_reduce(startb[:, :], past[:, :, :], AX.X, ALU.add)
                dve.drain()
                dve.tensor_tensor(rowf[:, :], block_no[:, :], startb[:, :], ALU.subtract)
                dve.drain()
                dve.tensor_scalar(startb[:, :], eb[:, :], float(REGION), None, ALU.mult)
                dve.drain()
                dve.scalar_tensor_tensor(out=rowf[:, :], in0=rowf[:, :], scalar=float(BLK), in1=startb[:, :],
                                         op0=ALU.mult, op1=ALU.add)
                dve.tensor_scalar(eb[:, :], eb[:, :], float(E - 1), None, ALU.min)
                dve.drain()
                dve.tensor_copy(row_i[:, :], rowf[:, :])
                dve.tensor_copy(exp_i[:, :], eb[:, :])
                dve.tensor_copy(base[:, :], region0[:, :])

            def block_mult(n, u):
                dve.wait_ge(s_esil, n + 1)
                at = 1536 * u + NC * BLK
                dve.scalar_tensor_tensor(out=eh32[u][:, :], in0=PSUM[:, at:at + NC * BLK], scalar=2.0 ** (SH - SX - SWT),
                                         in1=esil[u][:, :], op0=ALU.mult, op1=ALU.mult).then_inc(s_eh32, 1)

            def block_in(n, u, m):
                dve.wait_ge(s_et, n + 1)
                dve.tensor_scalar(second[:, :], xe[u][:, :, WORDS - 1], eb[:, bass.ds(m, 1)], float(T),
                                  ALU.not_equal, ALU.mult)
                dve.drain()
                dve.tensor_tensor(places[:, cols(m, HALVES)], second[:, :], xe[u][:, :, WORDS - 2], ALU.add)
                dve.tensor_copy(eT[u][:, :, :], PE_T[:, 0:2 * BLK].rearrange("p (a t) -> p a t", a=2)).then_inc(s_eT, 1)

            def block_low(n, u):
                dve.wait_ge(s_ehi, n + 1)
                low(ehT[u][:, 1, :, :], eh32[u][:, :].rearrange("p (c t) -> p c t", c=NC), ehT[u][:, 0, :, :], 0
                    ).then_inc(s_eh, 1)

            def experts(f):
                n0, n1 = f * NBLK, (f + 1) * NBLK

                def step(n, u, ahead=True):
                    if ahead:
                        block_in(n + 1, 1 - u, n + 1 - n0)
                    block_low(n - 1, 1 - u)
                    block_mult(n, u)

                block_in(n0, 0, 0)
                block_in(n0 + 1, 1, 1)
                block_mult(n0, 0)
                block_in(n0 + 2, 0, 2)
                block_low(n0, 0)
                block_mult(n0 + 1, 1)
                with dve.Fori(0, (NBLK - 4) // 2) as i:
                    step(i * 2 + (n0 + 2), 0)
                    step(i * 2 + (n0 + 3), 1)
                step(n1 - 2, 0)
                step(n1 - 1, 1, ahead=False)
                block_low(n1 - 1, 1)

            def combine(n, u, g):
                dve.wait_ge(s_Y[u], (n - u) * (16 * K // 2) + 16 * K)
                xs = X3(g)
                for k in range(K):
                    for j in range(NJ):
                        dve.scalar_tensor_tensor(out=xs[:, j, :], in0=Y[u][:, k, j, :],
                                                 scalar=PR[:, cols(g, NJ * K, j * K + k, 1)], in1=xs[:, j, :],
                                                 op0=ALU.mult, op1=ALU.add)
                    if k == 0:
                        dve.drain()
                dve.drain().then_inc(s_comb, 1)

            def attention(m):
                normalize(1, m, m, xn[:, 1, :]).then_inc(s_axn, 1)
                dve.wait_ge(s_ahi, m + 1)
                low(xa[:, 1, :, :], xn[:, 1, :].rearrange("p (j d) -> p j d", j=NJ), xa[:, 0, :, :], SX).then_inc(s_alo, 1)
                for q in range(2):
                    dve.wait_ge(s_qkv, m * 2 + (q + 1))
                    for a in range(2):
                        last = dve.scalar_tensor_tensor(out=qkv[:, a, :], in0=[PG, PU][a][:, 0:3 * D],
                                                        scalar=2.0 ** -(SX + SWT), in1=bias_a[:, :], op0=ALU.mult, op1=ALU.add)
                    last.then_inc(s_qkvb, 1)
                    dve.wait_ge(s_ex, m * 2 + (q + 1))
                    dve.scalar_tensor_tensor(out=qkv[:, :, 0:2 * D], in0=qkv[:, :, 0:2 * D], scalar=0.0, in1=relu[:, :, :],
                                             op0=ALU.max, op1=ALU.add).then_inc(s_phi, 1)
                    for a in range(2):
                        j = 2 * q + a
                        dve.wait_ge(s_cum, m * 4 + (j + 1))
                        q4 = qkv[:, a, 0:D].rearrange("p (h i j) -> p h i j", h=HEADS, j=1).to_broadcast([P, HEADS, HD, HD])
                        dve.tensor_tensor(prod[:, :].rearrange("p (h i j) -> p h i j", h=HEADS, i=HD),
                                          PKV[:, 0:KVW].rearrange("p (h i j) -> p h i j", h=HEADS, i=HD), q4, ALU.mult)
                        dve.tensor_tensor(prodk[:, :], PKV[:, KVW:KVW + D], qkv[:, a, 0:D], ALU.mult).then_inc(s_cumu, 1)
                        dve.drain()
                        dve.tensor_reduce(num[:, :].rearrange("p (h j) -> p h j", h=HEADS),
                                          prod[:, :].rearrange("p (h i j) -> p h j i", h=HEADS, i=HD), AX.X, ALU.add)
                        dve.tensor_reduce(den[:, :], prodk[:, :].rearrange("p (h i) -> p h i", h=HEADS), AX.X, ALU.add)
                        dve.drain()
                        dve.tensor_scalar(den[:, :], den[:, :], EPS_DEN, None, ALU.add)
                        dve.drain()
                        dve.reciprocal(rden[:, :], den[:, :])
                        dve.drain()
                        dve.tensor_tensor(y32[:, j, :].rearrange("p (h j) -> p h j", h=HEADS),
                                          num[:, :].rearrange("p (h j) -> p h j", h=HEADS),
                                          rden[:, :].rearrange("p (h j) -> p h j", j=1).to_broadcast([P, HEADS, HD]), ALU.mult)
                dve.drain().then_inc(s_y32, 1)
                dve.wait_ge(s_yhi, m + 1)
                low(ya[:, 1, :, :], y32[:, :, :], ya[:, 0, :, :], SY).then_inc(s_ylo, 1)
                dve.wait_ge(s_ao, m + 1)
                xg = X[:, cols(m, GT)]
                dve.scalar_tensor_tensor(out=xg, in0=PO[:, :], scalar=2.0 ** -(SY + SWT), in1=xg, op0=ALU.mult, op1=ALU.add)
                dve.drain()
                dve.tensor_tensor(X3(m), X3(m), bias_p[:, :].rearrange("p (j d) -> p j d", j=1).to_broadcast([P, NJ, D]),
                                  ALU.add)
                dve.drain().then_inc(s_adone, 1)

            dve.wait_ge(s_const2, 1)
            dve.tensor_copy(base[:, :], region0[:, :])
            dve.wait_ge(s_x0, 32)

            def route0(n, u):
                def ahead():
                    if not isinstance(n, int) or n < NG - 1:
                        if isinstance(n, int) and n > 0:
                            dve.wait_ge(s_x1, 16 * (NG - 2))
                        statistics(0, n + 1)
                route(n, u, n, ahead)

            statistics(0, 0)
            pairs(dve, 0, NG, route0)
            tables(0)
            phase_end(dve, 1)
            experts(0)
            phase_end(dve, 2)

            def both(n, u):
                m = n - NG

                def ahead():
                    if not isinstance(n, int) or n < 2 * NG - 1:
                        combine(m + 1, 1 - u, m + 1)
                        statistics(1, m + 1)
                attention(m)
                statistics(0, m)
                route(n, u, m, ahead)

            combine(0, 0, 0)
            statistics(1, 0)

            pairs(dve, NG, 2 * NG, both)
            tables(1)
            phase_end(dve, 3)
            experts(1)
            phase_end(dve, 4)
            pairs(dve, NG, 2 * NG, lambda n, u: combine(n, u, n - NG))


_INS = ['L0_attn_x', 'L0_attn_W_attn', 'L0_attn_b_attn', 'L0_attn_W_proj', 'L0_attn_b_proj', 'L0_ffn_gate_w',
        'L0_ffn_Wg', 'L0_ffn_Wu', 'L0_ffn_Wd', 'L0_ffn_Sg', 'L0_ffn_Su', 'L0_ffn_Sd']


def kernel(**inputs):
    import numpy as _np
    import concourse.bacc as _bacc
    from concourse import mybir as _mybir
    from concourse.bass_utils import run_bass_kernel_spmd as _run

    nc = _bacc.Bacc("TRN2", target_bir_lowering=False, num_devices=1)
    arrays, args = {}, []
    for name in _INS:
        a = _np.ascontiguousarray(inputs[name])
        if name == 'L0_attn_x':
            a = a.reshape(T, D)
        arrays[f"in_{name}_dram"] = a
        args.append(nc.dram_tensor(f"in_{name}_dram", a.shape, _mybir.dt.from_np(a.dtype), kind="ExternalInput").ap())
    args.append(nc.dram_tensor("out_0_dram", (T, D), _mybir.dt.float32, kind="ExternalOutput").ap())
    macaron(nc, *args)
    r = _run(nc, [arrays], core_ids=[0])
    return r.results[0]["out_0_dram"].reshape(B, S, D)
```

```python
from contextlib import ExitStack

import concourse.bass as bass
from concourse import mybir

F32, F16, I32, U32 = mybir.dt.float32, mybir.dt.float16, mybir.dt.int32, mybir.dt.uint32
ALU = mybir.AluOpType
ACT = mybir.ActivationFunctionType
AX = mybir.AxisListType

P = 128
D = 128
E = 8
K = 2
FI = 352
FS = 176
B, S = 32, 256
T = B * S
TILE = P
NJ = 4
GT = NJ * TILE
NG = T // GT
HEADS, HD = 16, 8
BLK = 256
HALVES = BLK // P
NBLK = T * K // BLK + E
NC = 3
FP = NC * P
SC = 2
UNITS = SC * 2
SW = FS // SC
REGION = T + BLK
ROWS = E * REGION + E * BLK
WORDS = 130
NOTOK = float(1 << 20)

SX, SWT, SH, SY, SBIAS = 10, 8, 2, 4, 10
EPS_LN, EPS_DEN = 1e-5, 1e-6
VD = HD + 1
KVW = HEADS * HD * VD
PHASES = 5


def macaron(nc, x, w_attn, b_attn, w_proj, b_proj, gate_w, wg, wu, wd, sg, su, sd, out):
    ctx = ExitStack()
    with ctx:
        def sb(name, shape, dt=F32):
            return ctx.enter_context(nc.sbuf_tensor(name, shape, dt))

        def ps(name, shape, dt=F32):
            return ctx.enter_context(nc.psum_tensor(name, shape, dt))

        def sem(name):
            return ctx.enter_context(nc.semaphore(name))

        routed = nc.dram_tensor("routed_rows", (ROWS, WORDS), F32).ap()
        result = nc.dram_tensor("expert_results", (K * T, D), F32).ap()

        X = sb("X", [P, T // P * D])
        PR = sb("PR", [P, NG * NJ * K])
        WG = sb("WG", [P, 2, E * FP], F16)
        WU = sb("WU", [P, 2, E * FP], F16)
        WD = sb("WD", [P, 2, E * NC * D], F16)
        GW = sb("GW", [P, 2, E], F16)
        SGW = sb("SGW", [P, 2, FS], F16)
        SUW = sb("SUW", [P, 2, FS], F16)
        SDW = sb("SDW", [P, 2, SC * D], F16)
        AW = sb("AW", [P, 2, 3 * D], F16)
        PW = sb("PW", [P, 2, D], F16)
        WSIZE = E * NC * D
        space = sb("space", [P, 3 * WSIZE])
        expert_w = [space[:, w * WSIZE:(w + 1) * WSIZE] for w in range(3)]
        taken = [0]

        def reused(pattern, **sizes):
            n, at = 1, taken[0]
            for size in sizes.values():
                n *= size
            taken[0] += n
            return space[:, at:at + n].rearrange(pattern, **sizes)

        small_w = sb("small_w", [P, 2 * FS + SC * D + 4 * D + E])
        bias_f = sb("bias_f", [P, 4 * D])
        bias_l = sb("bias_l", [P, 4 * D], F16)
        bias = sb("bias", [P, 4 * D], F16)
        rows_a = sb("rows_a", [P, P], F16)
        rows_p = sb("rows_p", [P, P], F16)
        ident = sb("ident", [P, P], F16)
        before = sb("before", [P, P], F16)
        ones16 = sb("ones16", [P, P], F16)
        upto = sb("upto", [P, P])
        ones32 = sb("ones32", [P, P])
        lower = sb("lower", [P, NJ, E, E])
        expert_no = sb("expert_no", [P, NJ, E])
        block_no = sb("block_no", [P, NBLK])
        base = sb("base", [P, E])
        base_i = sb("base_i", [P, E], I32)
        region0 = sb("region0", [P, E])
        pad_rows = sb("pad_rows", [P, HALVES, WORDS])
        xn = sb("xn", [P, 2, NJ, D])
        stats = sb("stats", [P, 2, NJ, 6])
        mv = sb("mv", [P, 2, NJ, 2])
        var = sb("var", [P, 2, NJ])
        rstd = sb("rstd", [P, 2, NJ])
        shift = sb("shift", [P, 2, NJ])
        newton = sb("newton", [P, 2, NJ])
        row = [sb(f"row{u}", [P, NJ, WORDS]) for u in range(2)]
        xT = [sb(f"xT{u}", [P, 2, GT], F16) for u in range(2)]
        lg = sb("lg", [P, NJ, E])
        better = sb("better", [P, NJ, E, E])
        equal = sb("equal", [P, NJ, E, E])
        rank = sb("rank", [P, NJ, E])
        pick = sb("pick", [P, K, NJ, E])
        chosen = sb("chosen", [P, NJ, E], F16)
        posb = sb("posb", [P, NJ, E])
        pk = sb("pk", [P, K, NJ, E])
        vtop = sb("vtop", [P, K, NJ])
        th = sb("th", [P, NJ])
        dstf = [sb(f"dstf{u}", [P, K, NJ]) for u in range(2)]
        dstc = sb("dstc", [P, K, NJ])
        idx = [sb(f"idx{u}", [P, K, NJ], U32) for u in range(2)]
        ssil = sb("ssil", [SW, SC, GT])
        sh32 = sb("sh32", [SW, SC, GT])
        shT = sb("shT", [SW, 2, SC, GT], F16)
        nb = sb("nb", [P, E])
        nbi = sb("nbi", [P, E], I32)
        cum = sb("cum", [P, E])
        past = sb("past", [P, NBLK, E])
        eb = sb("eb", [P, NBLK])
        startb = sb("startb", [P, NBLK])
        rowf = sb("rowf", [P, NBLK])
        row_i = sb("row_i", [P, NBLK], I32)
        exp_i = sb("exp_i", [P, NBLK], I32)
        xe = [sb(f"xe{u}", [P, HALVES, WORDS]) for u in range(2)]
        eT = [sb(f"eT{u}", [P, 2, BLK], F16) for u in range(2)]
        esil = [sb(f"esil{u}", [P, NC * BLK]) for u in range(2)]
        eh32 = [sb(f"eh32{u}", [P, NC * BLK]) for u in range(2)]
        ehT = [sb(f"ehT{u}", [P, 2, NC, BLK], F16) for u in range(2)]
        ey = [sb(f"ey{u}", [P, HALVES, D]) for u in range(2)]
        second = sb("second", [P, 2, HALVES])
        places = sb("places", [P, NBLK * HALVES])
        eidx = [sb(f"eidx{u}", [P, HALVES], U32) for u in range(2)]
        carrier = sb("carrier", [P, 2])
        Y = [reused("p (k j d) -> p k j d", k=K, j=NJ, d=D) for u in range(2)]
        xa = sb("xa", [P, 2, NJ, D], F16)
        xaT = sb("xaT", [P, 2, GT], F16)
        relu = reused("p (q a d) -> p q a d", q=2, a=2, d=2 * D)
        expo = sb("expo", [P, 2, 2, 2 * D])
        qk = sb("qk", [P, 2, 2, 2 * D])
        val = sb("val", [P, 2, 2, HEADS, VD])
        kv = reused("p (q a w) -> p q a w", q=2, a=2, w=KVW)
        prod = sb("prod", [P, 2, KVW])
        num = reused("p (j h v) -> p j h v", j=NJ, h=HEADS, v=VD)
        rden = sb("rden", [P, NJ, HEADS])
        y32 = reused("p (j d) -> p j d", j=NJ, d=D)
        ya = sb("ya", [P, 2, NJ, D], F16)
        yaT = sb("yaT", [P, 2, GT], F16)

        is_row = sb("is_row", [P, 2])
        f_state = [0]

        PSUM = ps("PSUM", [P, 8 * 512])

        def bank(n, m=1):
            return PSUM[:, 512 * n:512 * (n + m)]

        PT = bank(0).bitcast(F16)
        PL = bank(1)
        PG = [bank(2), bank(3)]
        PO = bank(4)
        KV0 = (3 * 512 - KVW) // 2
        PKV = bank(5, 3)[:, KV0:KV0 + KVW]
        PE_T = bank(7).bitcast(F16)
        PE_Y = bank(6)

        s_load0, s_x0, s_x1 = sem("s_load0"), sem("s_x0"), sem("s_x1")
        s_const, s_const2, s_wprep, s_whi = sem("s_const"), sem("s_const2"), sem("s_wprep"), sem("s_whi")
        s_wload, s_zero = [sem(f"s_wload{w}") for w in range(3)], sem("s_zero")
        s_phase = sem("s_phase")
        s_xn, s_hi, s_lo, s_pt, s_xT = sem("s_xn"), sem("s_hi"), sem("s_lo"), sem("s_pt"), sem("s_xT")
        s_lg, s_chosen, s_pos, s_route = sem("s_lg"), sem("s_chosen"), sem("s_pos"), sem("s_route")
        s_vtop, s_th = sem("s_vtop"), sem("s_th")
        s_sgu, s_ssil, s_sh32, s_shhi, s_sh, s_so, s_sdone = (
            sem("s_sgu"), sem("s_ssil"), sem("s_sh32"), sem("s_shhi"), sem("s_sh"), sem("s_so"), sem("s_sdone"))
        s_scat = [sem("s_scat0"), sem("s_scat1")]
        s_base, s_pad, s_tab = sem("s_base"), sem("s_pad"), sem("s_tab")
        s_xe = [sem("s_xe0"), sem("s_xe1")]
        s_et, s_eT, s_egu, s_esil, s_eh32, s_ehi, s_eh, s_ey, s_eyb, s_placed = (
            sem("s_et"), sem("s_eT"), sem("s_egu"), sem("s_esil"), sem("s_eh32"), sem("s_ehi"), sem("s_eh"),
            sem("s_ey"), sem("s_eyb"), sem("s_placed"))
        s_carrier = sem("s_carrier")
        s_res = [sem("s_res0"), sem("s_res1")]
        s_Y = [sem("s_Y0"), sem("s_Y1")]
        s_comb, s_weighed, s_dev = sem("s_comb"), sem("s_weighed"), sem("s_dev")
        s_axn, s_ahi, s_alo, s_at, s_aT = sem("s_axn"), sem("s_ahi"), sem("s_alo"), sem("s_at"), sem("s_aT")
        s_qkv, s_qkvb, s_phi, s_kv, s_cum, s_cumu = (
            sem("s_qkv"), sem("s_qkvb"), sem("s_phi"), sem("s_kv"), sem("s_cum"), sem("s_cumu"))
        s_y32, s_yhi, s_ylo, s_yt, s_yT, s_ao, s_adone = (
            sem("s_y32"), sem("s_yhi"), sem("s_ylo"), sem("s_yt"), sem("s_yT"), sem("s_ao"), sem("s_adone"))
        s_out = sem("s_out")

        def wait(eng, s, v):
            if not isinstance(v, int) or v > 0:
                eng.wait_ge(s, v)

        def phase_end(eng, n):
            eng.drain().then_inc(s_phase, 1)
            eng.wait_ge(s_phase, PHASES * n)

        def pairs(eng, first, last, step):
            step(first, 0)
            step(first + 1, 1)
            with eng.Fori(0, (last - first) // 2 - 2) as i:
                step(i * 2 + (first + 2), 0)
                step(i * 2 + (first + 3), 1)
            step(last - 2, 0)
            step(last - 1, 1)

        def streams_of(eng, step):
            step(-2, 0, False, False, True)
            step(-1, 1, False, True, True)
            step(0, 0, True, True, True)
            with eng.Fori(0, (NG - 4) // 2) as i:
                step(i * 2 + 1, 1, True, True, True)
                step(i * 2 + 2, 0, True, True, True)
            step(NG - 3, 1, True, True, True)
            step(NG - 2, 0, True, True, False)
            step(NG - 1, 1, True, False, False)

        def SLOT(n, u):
            first = f_state[0] == 0
            return u if first else 0

        def cols(n, width, at=0, size=None):
            return bass.ds(n * width + at, width if size is None else size)

        def X3(n):
            return X[:, cols(n, GT)].rearrange("p (j d) -> p j d", j=NJ)

        block = ctx.enter_context(nc.Block())

        @block.sync
        def _(sp):
            def tokens(ap, g):
                return ap[g * GT:(g + 1) * GT, :].rearrange("(j p) d -> p j d", p=P)

            sp.dma_start(X3(0), tokens(x, 0)).then_inc(s_x0, 16)
            sp.dma_start(X3(1), tokens(x, 1)).then_inc(s_x0, 16)
            o = 0
            for w, n in ((gate_w, E), (sg, FS), (su, FS), (w_attn, 3 * D), (w_proj, D)):
                sp.dma_start(small_w[:, o:o + n], w).then_inc(s_load0, 16)
                o += n
            for c in range(SC):
                sp.dma_start(small_w[0:SW, o:o + D], sd[c * SW:(c + 1) * SW, :]).then_inc(s_load0, 16)
                o += D
            sp.wait_ge(s_zero, 1)
            for r in range(2):
                sp.dma_start(bias_f[r:r + 1, 0:3 * D], b_attn.rearrange("(a n) -> a n", a=1)).then_inc(s_load0, 16)
                sp.dma_start(bias_f[r:r + 1, 3 * D:4 * D], b_proj.rearrange("(a n) -> a n", a=1)).then_inc(s_load0, 16)
            for g in range(2, NG):
                sp.dma_start(X3(g), tokens(x, g)).then_inc(s_x1, 16)
            for n, w in enumerate((wg, wu)):
                sp.dma_start(expert_w[n][:, 0:E * FI].rearrange("p (e i) -> p e i", e=E),
                             w.rearrange("e h i -> h e i")).then_inc(s_wload[n], 16)
            v = expert_w[2][:, :].rearrange("p (e c h) -> p e c h", e=E, c=NC)
            for c in range(NC):
                k = min(P, FI - c * P)
                sp.dma_start(v[0:k, :, c, :], wd[:, c * P:c * P + k, :].rearrange("e k h -> k e h")
                             ).then_inc(s_wload[2], 16)

            def pads(f):
                wait(sp, s_base, f + 1)
                for e in range(E):
                    at = sp.value_load(base_i[0:1, e:e + 1], min_val=e * REGION, max_val=e * REGION + T)
                    sp.dma_start(routed[bass.ds(at, BLK), :].rearrange("(h p) w -> p h w", p=P),
                                 pad_rows[:, :, :]).then_inc(s_pad, 16)
                sp.wait_ge(s_pad, 16 * (E * (f + 2)))

            def load_block(f):
                def step(n, u):
                    m = n - f * NBLK
                    wait(sp, s_eT, n - 1)
                    wait(sp, s_placed, n - 1)
                    at = sp.value_load(row_i[0:1, bass.ds(m, 1)], min_val=0, max_val=ROWS - BLK)
                    sp.dma_start(xe[u][:, :, :], routed[bass.ds(at, BLK), :].rearrange("(h p) w -> p h w", p=P)
                                 ).then_inc(s_xe[u], 16)
                return step

            def load_results(n, u):
                wait(sp, s_comb, n - 1)
                for k in range(K):
                    g = n % NG if isinstance(n, int) else n - n_off[0]
                    sp.dma_start(Y[u][:, k, :, :],
                                 result[bass.ds(g * GT + k * T, GT), :].rearrange("(j p) d -> p j d", p=P)
                                 ).then_inc(s_Y[u], 16)

            sp.wait_ge(s_const, 1)
            for e in range(E):
                sp.dma_start(routed[E * REGION + e * BLK:E * REGION + (e + 1) * BLK, :].rearrange("(h p) w -> p h w", p=P),
                             pad_rows[:, :, :]).then_inc(s_pad, 16)
            n_off = [0]
            for f in range(2):
                pads(f)
                phase_end(sp, 2 * f + 1)
                pairs(sp, f * NBLK, (f + 1) * NBLK, load_block(f))
                phase_end(sp, 2 * f + 2)
                n_off[0] = f * NG
                if f == 0:
                    pairs(sp, 0, NG, load_results)

            def store(n, u):
                g = n - NG
                sp.wait_ge(s_comb, n + 1)
                sp.dma_start(out[bass.ds(g * GT, GT), :].rearrange("(j p) d -> p j d", p=P), X3(g)).then_inc(s_out, 16)

            load_results(NG, 0)
            load_results(NG + 1, 1)
            with sp.Fori(0, NG // 2 - 1) as i:
                for u in range(2):
                    store(i * 2 + (NG + u), u)
                    load_results(i * 2 + (NG + 2 + u), u)
            for u in range(2):
                store(2 * NG - 2 + u, u)
            sp.wait_ge(s_out, 16 * NG)

        @block.gpsimd
        def _(pool):
            pool.memset(bias_f[:, :], 0.0)
            pool.drain().then_inc(s_zero, 1)
            pool.memset(ones16[:, :], 1.0)
            pool.memset(rows_a[:, :], 0.0)
            pool.memset(rows_p[:, :], 0.0)
            pool.memset(ones32[:, :], 1.0)
            pool.memset(ident[:, :], 0.0)
            pool.memset(is_row[:, :], 0.0)
            pool.memset(lower[:, :, :, :], 1.0)
            pool.memset(pad_rows[:, :, :], 0.0)
            pool.drain()
            pool.memset(pad_rows[:, :, WORDS - 2:WORDS - 1], NOTOK)
            pool.memset(rows_a[0:2, :], 2.0 ** (SX + SWT - SBIAS))
            pool.memset(rows_p[0:2, :], 2.0 ** (SY + SWT - SBIAS))
            pool.drain().then_inc(s_const, 1)
            pool.affine_select(out=ident[:, :], in_=ident[:, :], compare_op=ALU.not_equal, fill=1.0, base=0,
                               pattern=[[-1, P]], channel_multiplier=1)
            pool.affine_select(out=before[:, :], in_=ones16[:, :], compare_op=ALU.is_gt, fill=0.0, base=0,
                               pattern=[[1, P]], channel_multiplier=-1)
            pool.affine_select(out=upto[:, :], in_=ones32[:, :], compare_op=ALU.is_ge, fill=0.0, base=0,
                               pattern=[[1, P]], channel_multiplier=-1)
            pool.affine_select(out=lower[:, :, :, :], in_=lower[:, :, :, :], compare_op=ALU.is_gt, fill=0.0, base=0,
                               pattern=[[0, NJ], [1, E], [-1, E]], channel_multiplier=0)
            pool.affine_select(out=is_row[:, :], in_=is_row[:, :], compare_op=ALU.not_equal, fill=1.0, base=0,
                               pattern=[[-1, 2]], channel_multiplier=1)
            pool.iota(expert_no[:, :, :], [[0, NJ], [1, E]], base=0, channel_multiplier=0,
                      allow_small_or_imprecise_dtypes=True)
            pool.iota(block_no[:, :], [[1, NBLK]], base=0, channel_multiplier=0,
                      allow_small_or_imprecise_dtypes=True)
            pool.iota(region0[:, :], [[REGION, E]], base=0, channel_multiplier=0,
                      allow_small_or_imprecise_dtypes=True)
            for u in range(2):
                pool.iota(row[u][:, :, WORDS - 2], [[TILE, NJ]], base=u * GT, channel_multiplier=1,
                          allow_small_or_imprecise_dtypes=True)
            pool.drain().then_inc(s_const2, 1)

            def scatter(n, u):
                pool.wait_ge(s_route, n + 1)
                pool.tensor_tensor(dstc[:, :, :], dstf[u][:, :, :],
                                   ones32[:, 0:K * NJ].rearrange("p (k j) -> p k j", k=K), ALU.mult)
                pool.drain()
                pool.tensor_copy(idx[u][:, :, :], dstc[:, :, :])
                pool.drain()
                for k in range(K):
                    for j in range(NJ):
                        pool.indirect_dma_start(routed, bass.IndirectOffsetOnAxis(ap=idx[u][:, k, j:j + 1], axis=0),
                                                row[u][:, j, :], None).then_inc(s_scat[u], 16)

            def results(n, u):
                pool.wait_ge(s_eyb, n + 1)
                pool.tensor_tensor(carrier[:, u:u + 1], ones32[:, 0:1], ones32[:, 0:1], ALU.mult).then_inc(s_carrier, 1)
                for h in range(HALVES):
                    pool.indirect_dma_start(result, bass.IndirectOffsetOnAxis(ap=eidx[u][:, h:h + 1], axis=0),
                                            ey[u][:, h, :], None, bounds_check=K * T - 1, oob_is_err=False
                                            ).then_inc(s_res[u], 16)

            def low(n, dst, slot, high, s_high, s_low):
                pool.wait_ge(s_high, n + 1)
                pool.tensor_tensor(dst, xn[:, slot, :, :], high, ALU.subtract).then_inc(s_low, 1)

            def outer(m, q, a):
                pool.wait_ge(s_phi, m * 2 + (q + 1))
                k4 = qk[:, q, a, D:2 * D].rearrange("p (h i j) -> p h i j", h=HEADS, j=1).to_broadcast([P, HEADS, HD, VD])
                v4 = val[:, q, a, :, :].rearrange("p h (i j) -> p h i j", i=1).to_broadcast([P, HEADS, HD, VD])
                pool.tensor_tensor(kv[:, q, a, :].rearrange("p (h i j) -> p h i j", h=HEADS, i=HD), k4, v4, ALU.mult
                                   ).then_inc(s_kv, 1)

            def combine(g, u):
                pool.wait_ge(s_weighed, g + 1)
                for k in range(K):
                    pool.tensor_tensor(X3(g), X3(g), Y[u][:, k, :, :], ALU.add)
                    last = pool.drain()
                last.then_inc(s_comb, 1)

            def row_low(n, u):
                low(n, row[u][:, :, D // 2:D].bitcast(F16), SLOT(n, u), row[u][:, :, 0:D // 2].bitcast(F16), s_hi, s_lo)

            f_now = [0]
            for f in range(2):
                f_now[0] = f_state[0] = f
                if f == 0:
                    def step(n, u):
                        if not isinstance(n, int) or n < NG - 1:
                            row_low(n + 1, 1 - u)
                        scatter(n, u)
                    row_low(0, 0)
                    pairs(pool, 0, NG, step)
                else:
                    def step(m, u, route, attend, ready):
                        if attend:
                            outer(m + 1, 1, 0)
                        if route:
                            row_low(m + NG, u)
                        if attend:
                            outer(m + 1, 1, 1)
                        if ready:
                            low(m + 2, xa[:, 1, :, :], 1, xa[:, 0, :, :], s_ahi, s_alo)
                            if not (isinstance(m, int) and m == NG - 3):
                                combine(m + 3, 1 - u)
                            outer(m + 2, 0, 0)
                            outer(m + 2, 0, 1)
                        if route:
                            scatter(m + NG, u)
                    for q in range(2):
                        pool.memset(val[:, q, :, :, HD:VD], 1.0)
                    combine(0, 0)
                    streams_of(pool, step)
                for u in range(2):
                    pool.wait_ge(s_scat[u], 16 * K * NJ * NG // 2 * (f + 1))
                phase_end(pool, 2 * f + 1)
                pairs(pool, f * NBLK, (f + 1) * NBLK, results)
                for u in range(2):
                    pool.wait_ge(s_res[u], 16 * HALVES * NBLK // 2 * (f + 1))
                phase_end(pool, 2 * f + 2)

        @block.scalar
        def _(act):
            def part(dst, src):
                act.activation(dst, src, ACT.Copy, scale=float(2 ** SWT))

            act.wait_ge(s_load0, 16 * 11)
            act.wait_ge(s_wprep, 1)
            o = 0
            for w, n in ((GW, E), (SGW, FS), (SUW, FS), (AW, 3 * D), (PW, D)):
                part(w[:, 0, :], small_w[:, o:o + n])
                o += n
            part(SDW[0:SW, 0, :], small_w[0:SW, o:o + SC * D])
            act.activation(bias[:, :], bias_f[:, :], ACT.Copy, scale=2.0 ** SBIAS)
            act.drain().then_inc(s_whi, 1)

            def expert_weights(n):
                act.wait_ge(s_wload[n], 16 if n < 2 else 16 * NC)
                if n < 2:
                    W = (WG, WU)[n]
                    part(W[:, 0, :].rearrange("p (e i) -> p e i", e=E)[:, :, 0:FI],
                         expert_w[n][:, 0:E * FI].rearrange("p (e i) -> p e i", e=E))
                else:
                    v, w = (a.rearrange("p (e c h) -> p e c h", e=E, c=NC) for a in (expert_w[2][:, :], WD[:, 0, :]))
                    part(w[:, :, 0:NC - 1, :], v[:, :, 0:NC - 1, :])
                    part(w[0:FI - 2 * P, :, NC - 1, :], v[0:FI - 2 * P, :, NC - 1, :])
                act.drain().then_inc(s_whi, 1)

            def normalize(slot, g):
                xs = X3(g)
                for j in range(NJ):
                    act.activation(xn[:, slot, j, :], xs[:, j, :], ACT.Identity, scale=rstd[:, slot, j:j + 1],
                                   bias=shift[:, slot, j:j + 1])
                act.drain()

            def high(n, u, g):
                act.wait_ge(s_dev, n - u + 2 if f_state[0] == 0 else g + (NG + 3))
                wait(act, s_scat[u], (n - u) * (16 * K * NJ // 2))
                normalize(SLOT(n, u), g)
                act.activation(row[u][:, :, 0:D // 2].bitcast(F16), xn[:, SLOT(n, u), :, :], ACT.Copy).then_inc(s_hi, 1)

            def evacuate(n, u):
                act.wait_ge(s_pt, n + 1)
                act.activation(xT[u][:, :, :], PT[:, :].rearrange("p (a t) -> p a t", a=2), ACT.Copy).then_inc(s_xT, 1)

            def shared_silu(n, c, h):
                act.wait_ge(s_sgu, n * UNITS + (c * 2 + h + 1))
                act.activation(ssil[:, c, h * GT // 2:(h + 1) * GT // 2], PG[h][0:SW, 0:GT // 2], ACT.Silu,
                               scale=2.0 ** -(SX + SWT)).then_inc(s_ssil, 1)

            def shared_high(n):
                act.wait_ge(s_sh32, n * UNITS + UNITS)
                wait(act, s_so, n)
                act.activation(shT[:, 0, :, :], sh32[:, :, :], ACT.Copy).then_inc(s_shhi, 1)

            def tanh(n):
                act.wait_ge(s_vtop, n + 1)
                act.activation(th[:, :], vtop[:, 0, :], ACT.Tanh, scale=0.5 * 2.0 ** -(SX + SWT)).then_inc(s_th, 1)

            def norm_high(m):
                act.wait_ge(s_dev, m + (NG + 1))
                normalize(1, m)
                act.activation(xa[:, 0, :, :], xn[:, 1, :, :], ACT.Copy).then_inc(s_ahi, 1)

            def norm_evacuate(m):
                act.wait_ge(s_at, m + 1)
                act.activation(xaT[:, :, :], PT[:, :].rearrange("p (a t) -> p a t", a=2), ACT.Copy).then_inc(s_aT, 1)

            def features(m, q, a):
                act.wait_ge(s_qkv, m * NJ + (2 * q + a + 1))
                z = PG[a]
                act.activation(relu[:, q, a, :], z[:, 0:2 * D], ACT.Relu, scale=2.0 ** -(SX + SWT))
                act.activation(expo[:, q, a, :], z[:, 0:2 * D], ACT.Exp, scale=2.0 ** -(SX + SWT))
                act.activation(val[:, q, a, :, 0:HD], z[:, 2 * D:3 * D].rearrange("p (h j) -> p h j", h=HEADS), ACT.Copy,
                               scale=2.0 ** -(SX + SWT)).then_inc(s_qkvb, 1)

            def weigh(g, u):
                act.wait_ge(s_Y[u], (g - u) * (16 * K // 2) + 16 * K)
                for k in range(K):
                    for j in range(NJ):
                        last = act.activation(Y[u][:, k, j, :], Y[u][:, k, j, :], ACT.Copy,
                                              scale=PR[:, cols(g, NJ * K, j * K + k, 1)])
                last.then_inc(s_weighed, 1)

            def y_high(m):
                act.wait_ge(s_y32, m + 1)
                act.activation(ya[:, 0, :, :], y32[:, :, :], ACT.Copy, scale=float(2 ** SY)).then_inc(s_yhi, 1)

            def y_evacuate(m):
                act.wait_ge(s_yt, m + 1)
                act.activation(yaT[:, :, :], PT[:, :].rearrange("p (a t) -> p a t", a=2), ACT.Copy).then_inc(s_yT, 1)

            def silu(n, u):
                act.wait_ge(s_egu, n + 1)
                act.activation(esil[u][:, :], PSUM[:, 1536 * u:1536 * u + 768], ACT.Silu,
                               scale=2.0 ** -(SX + SWT)).then_inc(s_esil, 1)

            def hi(n, u):
                act.wait_ge(s_eh32, n + 1)
                act.activation(ehT[u][:, 0, :, :], eh32[u][:, :].rearrange("p (c t) -> p c t", c=NC), ACT.Copy
                               ).then_inc(s_ehi, 1)

            def results(n, u):
                act.wait_ge(s_ey, n + 1)
                wait(act, s_res[u], res_value(n, u))
                wait(act, s_carrier, n - 1)
                act.activation(eidx[u][:, :], places[:, cols(n - f_state[0] * NBLK, HALVES)], ACT.Copy)
                act.activation(ey[u][:, :, :], PE_Y[:, 0:BLK].rearrange("p (h d) -> p h d", h=HALVES), ACT.Copy,
                               scale=0.5 * 2.0 ** -(SH + SWT)).then_inc(s_eyb, 1)

            def res_value(n, u):
                return (n - u) * (16 * HALVES // 2)

            def experts(f):
                n0, n1 = f * NBLK, (f + 1) * NBLK

                def step(n, u):
                    silu(n, u)
                    hi(n - 1, 1 - u)
                    results(n - 2, u)

                silu(n0, 0)
                silu(n0 + 1, 1)
                hi(n0, 0)
                step(n0 + 2, 0)
                step(n0 + 3, 1)
                with act.Fori(0, (NBLK - 4) // 2) as i:
                    step(i * 2 + (n0 + 4), 0)
                    step(i * 2 + (n0 + 5), 1)
                hi(n1 - 1, 1)
                results(n1 - 2, 0)
                results(n1 - 1, 1)

            def first_ffn(n, u):
                edge = isinstance(n, int)
                for c in range(SC):
                    for h in range(2):
                        shared_silu(n, c, h)
                    if c == 0 and not (edge and n == NG - 1):
                        high(n + 1, 1 - u, n + 1)
                tanh(n)
                if not (edge and n == NG - 1):
                    evacuate(n + 1, 1 - u)
                shared_high(n)
                if edge and n < 2:
                    expert_weights(n)
                if edge and n == NG - 2:
                    expert_weights(2)

            def streams(m, u, route, attend, ready):
                n = m + NG
                if route:
                    high(n, u, m)
                if ready:
                    norm_high(m + 2)
                if route:
                    evacuate(n, u)
                if ready:
                    norm_evacuate(m + 2)
                    if not (isinstance(m, int) and m == NG - 3):
                        weigh(m + 3, 1 - u)
                    for q in range(2):
                        for a in range(2):
                            features(m + 2, q, a)
                if attend:
                    y_high(m + 1)
                if route:
                    tanh(n)
                    for h in range(2):
                        shared_silu(n, 0, h)
                if attend:
                    y_evacuate(m + 1)
                if route:
                    for h in range(2):
                        shared_silu(n, 1, h)
                    shared_high(n)

            f_state[0] = 0
            high(0, 0, 0)
            evacuate(0, 0)
            pairs(act, 0, NG, first_ffn)
            phase_end(act, 1)
            experts(0)
            phase_end(act, 2)
            f_state[0] = 1
            weigh(0, 0)
            streams_of(act, streams)
            phase_end(act, 3)
            experts(1)
            phase_end(act, 4)

        @block.tensor
        def _(pe):
            def product(dst, a, b, start=True, stop=True):
                pe.matmul(dst, a[0], b[0], start=start, stop=False)
                pe.matmul(dst, a[0], b[1], start=False, stop=False)
                return pe.matmul(dst, a[1], b[0], start=False, stop=stop)

            def transpose_group(src, s):
                for part in range(2):
                    for j in range(NJ):
                        mm = pe.transpose(PT[:, part * GT + j * P:part * GT + (j + 1) * P], src(part, j), ident[:, :])
                mm.then_inc(s, 1)

            def transposes(n, u, m=None):
                pe.wait_ge(s_lo, n + 1)
                if m is None:
                    wait(pe, s_xT, n)
                else:
                    pe.wait_ge(s_yT, m + 1)
                transpose_group(lambda part, j: row[u][:, j, part * D // 2:(part + 1) * D // 2].bitcast(F16), s_pt)

            def logits(n, u):
                pe.wait_ge(s_xT, n + 1)
                for j in range(NJ):
                    t = slice(j * P, (j + 1) * P)
                    for a, b in ((0, 0), (0, 1), (1, 0), (1, 1)):
                        mm = pe.matmul(PL[:, j * E:(j + 1) * E], xT[u][:, a, t], GW[:, b, :], start=(a + b == 0), stop=(a + b == 2))
                mm.then_inc(s_lg, 1)

            def gate_up(n, u, c, h, last=False):
                i = c * 2 + h
                if c == 1 or f_state[0] == 0 or last:
                    wait(pe, s_sh32, n * UNITS + (i - 1))
                w = slice(c * SW, (c + 1) * SW)
                t = slice(h * GT // 2, (h + 1) * GT // 2)
                xh = [xT[u][:, a, t] for a in range(2)]
                product(PG[h][0:SW, 0:GT // 2], [SGW[:, 0, w], SGW[:, 1, w]], xh)
                product(PG[h][0:SW, GT // 2:GT], [SUW[:, 0, w], SUW[:, 1, w]], xh).then_inc(s_sgu, 1)

            def positions(n):
                pe.wait_ge(s_chosen, n + 1)
                pos = PL[:, 64:64 + (NJ + 1) * E]
                ch = chosen[:, :, :].rearrange("p j e -> p (j e)")
                pe.matmul(pos[:, 0:NJ * E], before[:, :], ch, start=True, stop=False, skip_group_check=True)
                for d in range(1, NJ + 1):
                    mm = pe.matmul(pos[:, d * E:(NJ + 1) * E], ones16[:, :], ch[:, 0:(NJ + 1 - d) * E], start=False,
                                   stop=(d == NJ), skip_group_check=True)
                mm.then_inc(s_pos, 1)

            def down(n, m=None):
                pe.wait_ge(s_sh, n + 1)
                if m is None:
                    wait(pe, s_sdone, n)
                else:
                    pe.wait_ge(s_adone, m + 1)
                for j in range(NJ):
                    t = slice(j * P, (j + 1) * P)
                    for c in range(SC):
                        h = slice(c * D, (c + 1) * D)
                        mm = product(PO[:, j * D:(j + 1) * D], [shT[:, 0, c, t], shT[:, 1, c, t]],
                                     [SDW[0:SW, 0, h], SDW[0:SW, 1, h]], start=(c == 0), stop=(c == SC - 1))
                mm.then_inc(s_so, 1)

            def attention_transposes(m):
                pe.wait_ge(s_alo, m + 1)
                if not isinstance(m, int) or m > 1:
                    pe.wait_ge(s_xT, m + (NG - 1))
                transpose_group(lambda part, j: xa[:, part, j, :], s_at)

            def qkv_products(m, q, a):
                j = 2 * q + a
                if q == 0:
                    pe.wait_ge(s_aT, m + 1)
                    if not isinstance(m, int) or m > 2:
                        pe.wait_ge(s_sh32, (m + (NG - 2)) * UNITS)
                    else:
                        wait(pe, s_qkvb, m * NJ)
                else:
                    pe.wait_ge(s_qkvb, m * NJ + (a + 1))
                t = slice(j * P, (j + 1) * P)
                pe.matmul(PG[a][:, 0:3 * D], rows_a[:, :], bias[:, 0:3 * D], start=True, stop=False)
                product(PG[a][:, 0:3 * D], [xaT[:, 0, t], xaT[:, 1, t]], [AW[:, 0, :], AW[:, 1, :]], start=False
                        ).then_inc(s_qkv, 1)

            def running_sums(m, q, a):
                j = 2 * q + a
                pe.wait_ge(s_kv, m * NJ + (j + 1))
                wait(pe, s_cumu, m * NJ + j)
                for lo, hi in ((0, 512 - KV0), (512 - KV0, 1024 - KV0), (1024 - KV0, KVW)):
                    mm = pe.matmul(PKV[:, lo:hi], upto[:, :], kv[:, q, a, lo:hi], start=True, stop=(a == 0))
                    if a:
                        mm = pe.matmul(PKV[:, lo:hi], ones32[:, :], kv[:, q, 0, lo:hi], start=False, stop=True)
                mm.then_inc(s_cum, 1)

            def y_transposes(m, ready):
                pe.wait_ge(s_ylo, m + 1)
                if ready:
                    pe.wait_ge(s_aT, m + 2)
                transpose_group(lambda part, j: ya[:, part, j, :], s_yt)

            def project(m):
                pe.wait_ge(s_yT, m + 1)
                if not isinstance(m, int) or m > 1:
                    pe.wait_ge(s_sdone, m + (NG - 1))
                for j in range(NJ):
                    t = slice(j * P, (j + 1) * P)
                    pe.matmul(PO[:, j * D:(j + 1) * D], rows_p[:, :], bias[:, 3 * D:4 * D], start=True, stop=False)
                    mm = product(PO[:, j * D:(j + 1) * D], [yaT[:, 0, t], yaT[:, 1, t]], [PW[:, 0, :], PW[:, 1, :]],
                                 start=False)
                mm.then_inc(s_ao, 1)

            def block_transposes(n, u):
                pe.wait_ge(s_xe[u], (n - u) * 8 + 16)
                wait(pe, s_eT, n)
                for part in range(2):
                    for h in range(HALVES):
                        at = part * BLK + h * P
                        mm = pe.transpose(PE_T[:, at:at + P],
                                          xe[u][:, h, part * D // 2:(part + 1) * D // 2].bitcast(F16), ident[:, :])
                mm.then_inc(s_et, 1)

            def experts_of(m, count):
                return nc.values_load_multi_w_load_instructions(exp_i[0:1, bass.ds(m, count)], engines=[pe.engine],
                                                                min_val=0, max_val=E - 1,
                                                                skip_runtime_bounds_check_because="tables() clamps them")[1]

            def block_gate_up(n, u, e):
                pe.wait_ge(s_eT, n + 1)
                wait(pe, s_eh32, n - 1)
                for W, o in ((WG, 0), (WU, NC * BLK)):
                    for c in range(NC):
                        w = [W[:, a, bass.ds(e * FP + c * P, P)] for a in range(2)]
                        at = 1536 * u + o + c * BLK
                        mm = product(PSUM[:, at:at + BLK], w, [eT[u][:, 0, :], eT[u][:, 1, :]])
                mm.then_inc(s_egu, 1)

            def block_down(n, u, e):
                pe.wait_ge(s_eh, n + 1)
                wait(pe, s_eyb, n)
                for h in range(HALVES):
                    t = slice(h * P, (h + 1) * P)
                    for c in range(NC):
                        w = [WD[:, a, bass.ds(e * (NC * D) + c * D, D)] for a in range(2)]
                        mm = product(PE_Y[:, h * D:(h + 1) * D], [ehT[u][:, 0, c, t], ehT[u][:, 1, c, t]], w,
                                     start=(c == 0), stop=(c == NC - 1))
                mm.then_inc(s_ey, 1)

            def experts(f):
                n0, n1 = f * NBLK, (f + 1) * NBLK

                def step(n, u, e, e_down=None, ahead=True):
                    if ahead:
                        block_transposes(n + 1, 1 - u)
                    block_gate_up(n, u, e)
                    if e_down is not None:
                        block_down(n - 2, u, e_down)

                e = experts_of(0, 2)
                block_transposes(n0, 0)
                step(n0, 0, e[0])
                step(n0 + 1, 1, e[1])
                with pe.Fori(0, (NBLK - 4) // 4) as i:
                    e = experts_of(i * 4, 6)
                    for b in range(4):
                        step(i * 4 + (n0 + 2 + b), b % 2, e[b + 2], e[b])
                e = experts_of(NBLK - 4, 4)
                step(n1 - 2, 0, e[2], e[0])
                step(n1 - 1, 1, e[3], e[1], ahead=False)
                block_down(n1 - 2, 0, e[2])
                block_down(n1 - 1, 1, e[3])

            pe.wait_ge(s_const2, 1)
            pe.wait_ge(s_wprep, 2)

            def first_ffn(n, u):
                logits(n, u)
                for c in range(SC):
                    for h in range(2):
                        gate_up(n, u, c, h)
                if not isinstance(n, int) or n < NG - 1:
                    transposes(n + 1, 1 - u)
                positions(n)
                down(n)

            def streams(m, u, route, attend, ready):
                n = m + NG
                if attend:
                    running_sums(m + 1, 0, 1)
                    running_sums(m + 1, 1, 0)
                if route:
                    transposes(n, u, m)
                if ready:
                    attention_transposes(m + 2)
                if route:
                    logits(n, u)
                if attend:
                    running_sums(m + 1, 1, 1)
                if route:
                    positions(n)
                if ready:
                    for q in range(2):
                        for a in range(2):
                            qkv_products(m + 2, q, a)
                if route:
                    if ready:
                        pe.wait_ge(s_qkvb, (m + 2) * NJ + NJ)
                    for h in range(2):
                        gate_up(n, u, 0, h, last=not ready)
                if attend:
                    y_transposes(m + 1, ready)
                if route:
                    for h in range(2):
                        gate_up(n, u, 1, h)
                if attend:
                    project(m + 1)
                if ready:
                    running_sums(m + 2, 0, 0)
                if route:
                    down(n, m + 1 if attend else m)

            f_state[0] = 0
            transposes(0, 0)
            pairs(pe, 0, NG, first_ffn)
            phase_end(pe, 1)
            experts(0)
            phase_end(pe, 2)
            f_state[0] = 1
            streams_of(pe, streams)
            phase_end(pe, 3)
            experts(1)
            phase_end(pe, 4)

        @block.vector
        def _(dve):
            def low(dst, src, high, scale):
                return dve.scalar_tensor_tensor(out=dst, in0=src, scalar=float(2 ** scale), in1=high,
                                                op0=ALU.mult, op1=ALU.subtract)

            def e3(ap, n):
                return ap.rearrange("p (e i) -> p e i", e=E)[:, :, 0:n]

            for W in (WG, WU, WD):
                dve.memset(W[:, :, :].bitcast(F32), 0.0)
            dve.drain().then_inc(s_wprep, 1)

            dve.wait_ge(s_const2, 1)
            dve.wait_ge(s_whi, 1)
            o = 0
            for w, n in ((GW, E), (SGW, FS), (SUW, FS), (AW, 3 * D), (PW, D)):
                low(w[:, 1, :], small_w[:, o:o + n], w[:, 0, :], SWT)
                o += n
            low(SDW[0:SW, 1, :], small_w[0:SW, o:o + SC * D], SDW[0:SW, 0, :], SWT)
            low(bias_l[:, :], bias_f[:, :], bias[:, :], SBIAS)
            dve.drain()
            dve.tensor_scalar(bias_l[:, :], bias_l[:, :], is_row[:, 1:2], None, ALU.mult)
            dve.drain()
            dve.scalar_tensor_tensor(out=bias[:, :], in0=bias[:, :], scalar=is_row[:, 0:1], in1=bias_l[:, :],
                                     op0=ALU.mult, op1=ALU.add)
            dve.drain().then_inc(s_wprep, 1)

            def expert_weights(n):
                dve.wait_ge(s_whi, n + 2)
                if n < 2:
                    W = (WG, WU)[n]
                    low(e3(W[:, 1, :], FI), expert_w[n][:, 0:E * FI].rearrange("p (e i) -> p e i", e=E), e3(W[:, 0, :], FI), SWT)
                else:
                    v, h, l = (a.rearrange("p (e c h) -> p e c h", e=E, c=NC) for a in (expert_w[2][:, :], WD[:, 0, :], WD[:, 1, :]))
                    low(l[:, :, 0:NC - 1, :], v[:, :, 0:NC - 1, :], h[:, :, 0:NC - 1, :], SWT)
                    q = FI - 2 * P
                    low(l[0:q, :, NC - 1, :], v[0:q, :, NC - 1, :], h[0:q, :, NC - 1, :], SWT)

            def moments(slot, g):
                xs = X3(g)
                for j in range(NJ):
                    dve.bn_stats(stats[:, slot, j, :], xs[:, j, :])
                dve.drain()
                for j in range(NJ):
                    dve.bn_aggr(mv[:, slot, j, :], stats[:, slot, j, :])

            def deviations(count):
                v, y, a = var[:, :, :], rstd[:, :, :], newton[:, :, :]
                dve.drain()
                dve.tensor_scalar(v, mv[:, :, :, 1], EPS_LN, 2.0 ** (-2 * SX), ALU.add, ALU.mult)
                dve.drain()
                dve.tensor_single_scalar(a.bitcast(I32), v.bitcast(I32), 1, ALU.arith_shift_right)
                dve.drain()
                dve.tensor_scalar(y.bitcast(I32), a.bitcast(I32), -1.0, float(0x5f3759df), ALU.mult, ALU.add)
                dve.drain()
                for _ in range(3):
                    dve.tensor_tensor(a, y, y, ALU.mult)
                    dve.drain()
                    dve.scalar_tensor_tensor(out=a, in0=a, scalar=-0.5, in1=v, op0=ALU.mult, op1=ALU.mult)
                    dve.drain()
                    dve.scalar_tensor_tensor(out=y, in0=a, scalar=1.5, in1=y, op0=ALU.add, op1=ALU.mult)
                    dve.drain()
                dve.scalar_tensor_tensor(out=shift[:, :, :], in0=mv[:, :, :, 0], scalar=-1.0, in1=y, op0=ALU.mult,
                                         op1=ALU.mult).then_inc(s_dev, count)

            def choose(n, u, g):
                dve.wait_ge(s_lg, n + 1)
                dve.tensor_copy(lg[:, :, :], PL[:, 0:NJ * E].rearrange("p (j e) -> p j e", j=NJ))
                dve.drain()
                mine = lg[:, :, :].rearrange("p j (e f) -> p j e f", f=1).to_broadcast([P, NJ, E, E])
                theirs = lg[:, :, :].rearrange("p j (f e) -> p j f e", f=1).to_broadcast([P, NJ, E, E])
                dve.tensor_tensor(better[:, :, :, :], theirs, mine, ALU.is_gt)
                dve.tensor_tensor(equal[:, :, :, :], theirs, mine, ALU.is_equal)
                dve.drain()
                dve.tensor_tensor(equal[:, :, :, :], equal[:, :, :, :], lower[:, :, :, :], ALU.mult)
                dve.drain()
                dve.tensor_tensor(better[:, :, :, :], better[:, :, :, :], equal[:, :, :, :], ALU.add)
                dve.drain()
                dve.tensor_reduce(rank[:, :, :], better[:, :, :, :], AX.X, ALU.add)
                dve.drain()
                dve.tensor_scalar(chosen[:, :, :], rank[:, :, :], float(K), None, ALU.is_lt).then_inc(s_chosen, 1)
                for k in range(K):
                    dve.tensor_scalar(pick[:, k, :, :], rank[:, :, :], float(k), None, ALU.is_equal)
                dve.drain()
                lk = lg[:, :, :].rearrange("p (k j) e -> p k j e", k=1).to_broadcast([P, K, NJ, E])
                dve.tensor_tensor(pk[:, :, :, :], pick[:, :, :, :], lk, ALU.mult)
                dve.tensor_tensor(posb[:, :, :], pick[:, 0, :, :], expert_no[:, :, :], ALU.mult)
                dve.drain()
                dve.tensor_reduce(vtop[:, :, :], pk[:, :, :, :], AX.X, ALU.add)
                dve.tensor_reduce(row[u][:, :, WORDS - 1], posb[:, :, :], AX.X, ALU.add)
                if not isinstance(n, int) or n >= 2:
                    dve.tensor_scalar(row[u][:, :, WORDS - 2], row[u][:, :, WORDS - 2], float(2 * GT), None, ALU.add)
                dve.drain()
                dve.tensor_tensor(vtop[:, 0, :], vtop[:, 0, :], vtop[:, 1, :], ALU.subtract).then_inc(s_vtop, 1)

            def place(n, u, g):
                dve.wait_ge(s_pos, n + 1)
                pos = PL[:, 64:64 + (NJ + 1) * E].rearrange("p (j e) -> p j e", j=NJ + 1)
                bj = base[:, :].rearrange("p (j e) -> p j e", j=1).to_broadcast([P, NJ, E])
                dve.tensor_tensor(posb[:, :, :], pos[:, 0:NJ, :], bj, ALU.add)
                dve.drain()
                dve.tensor_tensor(base[:, :], base[:, :], pos[:, NJ, :], ALU.add)
                pb = posb[:, :, :].rearrange("p (k j) e -> p k j e", k=1).to_broadcast([P, K, NJ, E])
                dve.tensor_tensor(pk[:, :, :, :], pick[:, :, :, :], pb, ALU.mult)
                dve.drain()
                dve.tensor_reduce(dstf[u][:, :, :], pk[:, :, :, :], AX.X, ALU.add).then_inc(s_route, 1)
                dve.wait_ge(s_th, n + 1)
                pr = PR[:, cols(g, NJ * K)].rearrange("p (j k) -> p j k", k=K)
                for k in range(K):
                    dve.tensor_scalar(pr[:, :, k], th[:, :], 0.5 - k, 0.5, ALU.mult, ALU.add)

            def shared(n, c, h):
                dve.wait_ge(s_ssil, n * UNITS + (c * 2 + h + 1))
                t = slice(h * GT // 2, (h + 1) * GT // 2)
                dve.scalar_tensor_tensor(out=sh32[:, c, t], in0=PG[h][0:SW, GT // 2:GT], scalar=2.0 ** (SH - SX - SWT),
                                         in1=ssil[:, c, t], op0=ALU.mult, op1=ALU.mult).then_inc(s_sh32, 1)

            def shared_low(n):
                dve.wait_ge(s_shhi, n + 1)
                low(shT[:, 1, :, :], sh32[:, :, :], shT[:, 0, :, :], 0).then_inc(s_sh, 1)

            def shared_add(n, g):
                dve.wait_ge(s_so, n + 1)
                xg = X[:, cols(g, GT)]
                dve.scalar_tensor_tensor(out=xg, in0=PO[:, :], scalar=0.5 * 2.0 ** -(SH + SWT), in1=xg,
                                         op0=ALU.mult, op1=ALU.add).then_inc(s_sdone, 1)

            def tables(f):
                dve.drain()
                dve.tensor_copy(base_i[:, :], base[:, :]).then_inc(s_base, 1)
                dve.tensor_tensor(nb[:, :], base[:, :], region0[:, :], ALU.subtract)
                dve.drain()
                dve.tensor_scalar(nb[:, :], nb[:, :], float(BLK - 1), None, ALU.add)
                dve.drain()
                dve.tensor_copy(nbi[:, :], nb[:, :])
                dve.drain()
                dve.tensor_single_scalar(nbi[:, :], nbi[:, :], BLK.bit_length() - 1, ALU.arith_shift_right)
                dve.drain()
                dve.tensor_copy(nb[:, :], nbi[:, :])
                dve.drain()
                dve.tensor_copy(cum[:, 0:1], nb[:, 0:1])
                for e in range(1, E):
                    dve.drain()
                    dve.tensor_tensor(cum[:, e:e + 1], cum[:, e - 1:e], nb[:, e:e + 1], ALU.add)
                dve.drain()
                dve.tensor_tensor(past[:, :, :], block_no[:, :].rearrange("p (b e) -> p b e", e=1).to_broadcast([P, NBLK, E]),
                                  cum[:, :].rearrange("p (b e) -> p b e", b=1).to_broadcast([P, NBLK, E]), ALU.is_ge)
                dve.drain()
                dve.tensor_reduce(eb[:, :], past[:, :, :], AX.X, ALU.add)
                dve.drain()
                dve.tensor_tensor(past[:, :, :], past[:, :, :],
                                  nb[:, :].rearrange("p (b e) -> p b e", b=1).to_broadcast([P, NBLK, E]), ALU.mult)
                dve.drain()
                dve.tensor_reduce(startb[:, :], past[:, :, :], AX.X, ALU.add)
                dve.drain()
                dve.tensor_tensor(rowf[:, :], block_no[:, :], startb[:, :], ALU.subtract)
                dve.drain()
                dve.tensor_scalar(startb[:, :], eb[:, :], float(REGION), None, ALU.mult)
                dve.drain()
                dve.scalar_tensor_tensor(out=rowf[:, :], in0=rowf[:, :], scalar=float(BLK), in1=startb[:, :],
                                         op0=ALU.mult, op1=ALU.add)
                dve.tensor_scalar(eb[:, :], eb[:, :], float(E - 1), None, ALU.min)
                dve.drain()
                dve.tensor_copy(row_i[:, :], rowf[:, :])
                dve.tensor_copy(exp_i[:, :], eb[:, :])
                dve.tensor_copy(base[:, :], region0[:, :])

            def block_mult(n, u):
                dve.wait_ge(s_esil, n + 1)
                at = 1536 * u + NC * BLK
                dve.scalar_tensor_tensor(out=eh32[u][:, :], in0=PSUM[:, at:at + NC * BLK], scalar=2.0 ** (SH - SX - SWT),
                                         in1=esil[u][:, :], op0=ALU.mult, op1=ALU.mult).then_inc(s_eh32, 1)

            def block_in(n, u, m):
                dve.wait_ge(s_et, n + 1)
                dve.tensor_copy(eT[u][:, :, :], PE_T[:, 0:2 * BLK].rearrange("p (a t) -> p a t", a=2)).then_inc(s_eT, 1)
                dve.tensor_scalar(second[:, u, :], xe[u][:, :, WORDS - 1], eb[:, bass.ds(m, 1)], float(T),
                                  ALU.not_equal, ALU.mult)
                dve.drain()
                dve.tensor_tensor(places[:, cols(m, HALVES)], second[:, u, :], xe[u][:, :, WORDS - 2], ALU.add).then_inc(s_placed, 1)

            def block_low(n, u):
                dve.wait_ge(s_ehi, n + 1)
                low(ehT[u][:, 1, :, :], eh32[u][:, :].rearrange("p (c t) -> p c t", c=NC), ehT[u][:, 0, :, :], 0
                    ).then_inc(s_eh, 1)

            def experts(f):
                n0, n1 = f * NBLK, (f + 1) * NBLK

                def step(n, u, ahead=True):
                    if ahead:
                        block_in(n + 1, 1 - u, n + 1 - n0)
                    block_low(n - 1, 1 - u)
                    block_mult(n, u)

                block_in(n0, 0, 0)
                block_in(n0 + 1, 1, 1)
                block_mult(n0, 0)
                block_in(n0 + 2, 0, 2)
                block_low(n0, 0)
                block_mult(n0 + 1, 1)
                with dve.Fori(0, (NBLK - 4) // 2) as i:
                    step(i * 2 + (n0 + 2), 0)
                    step(i * 2 + (n0 + 3), 1)
                step(n1 - 2, 0)
                step(n1 - 1, 1, ahead=False)
                block_low(n1 - 1, 1)

            def combine(n, u, g):
                dve.wait_ge(s_Y[u], (n - u) * (16 * K // 2) + 16 * K)
                xs = X3(g)
                for k in range(K):
                    for j in range(NJ):
                        dve.scalar_tensor_tensor(out=xs[:, j, :], in0=Y[u][:, k, j, :],
                                                 scalar=PR[:, cols(g, NJ * K, j * K + k, 1)], in1=xs[:, j, :],
                                                 op0=ALU.mult, op1=ALU.add)
                    if k == 0:
                        dve.drain()
                dve.drain().then_inc(s_comb, 1)

            def features(m, q):
                dve.wait_ge(s_qkvb, m * NJ + (2 * q + 2))
                dve.scalar_tensor_tensor(out=qk[:, q, :, :], in0=expo[:, q, :, :], scalar=1.0, in1=relu[:, q, :, :],
                                         op0=ALU.min, op1=ALU.add).then_inc(s_phi, 1)

            def attend(m, q, a):
                j = 2 * q + a
                dve.wait_ge(s_cum, m * NJ + (j + 1))
                q4 = qk[:, q, a, 0:D].rearrange("p (h i j) -> p h i j", h=HEADS, j=1).to_broadcast([P, HEADS, HD, VD])
                dve.tensor_tensor(prod[:, a, :].rearrange("p (h i j) -> p h i j", h=HEADS, i=HD),
                                  PKV[:, :].rearrange("p (h i j) -> p h i j", h=HEADS, i=HD), q4, ALU.mult).then_inc(s_cumu, 1)
                dve.drain()
                dve.tensor_reduce(num[:, j, :, :], prod[:, a, :].rearrange("p (h i j) -> p h j i", h=HEADS, i=HD),
                                  AX.X, ALU.add)

            def divide(m):
                dve.drain()
                dve.tensor_scalar(rden[:, :, :], num[:, :, :, HD], EPS_DEN, None, ALU.add)
                dve.drain()
                dve.reciprocal(rden[:, :, :], rden[:, :, :])
                dve.drain()
                dve.tensor_tensor(y32[:, :, :].rearrange("p j (h i) -> p j h i", h=HEADS), num[:, :, :, 0:HD],
                                  rden[:, :, :].rearrange("p j (h i) -> p j h i", i=1).to_broadcast([P, NJ, HEADS, HD]),
                                  ALU.mult).then_inc(s_y32, 1)

            def y_low(m):
                dve.wait_ge(s_yhi, m + 1)
                low(ya[:, 1, :, :], y32[:, :, :], ya[:, 0, :, :], SY).then_inc(s_ylo, 1)

            def attention_add(m):
                dve.wait_ge(s_ao, m + 1)
                xg = X[:, cols(m, GT)]
                dve.scalar_tensor_tensor(out=xg, in0=PO[:, :], scalar=2.0 ** -(SY + SWT), in1=xg, op0=ALU.mult,
                                         op1=ALU.add).then_inc(s_adone, 1)
                dve.drain()

            dve.tensor_copy(base[:, :], region0[:, :])
            dve.wait_ge(s_x0, 32)

            def first_ffn(n, u):
                edge = isinstance(n, int)
                choose(n, u, n)
                for c in range(SC):
                    for h in range(2):
                        shared(n, c, h)
                place(n, u, n)
                if u == 0 and not (edge and n == NG - 2):
                    dve.wait_ge(s_hi, n + 2)
                    if edge and n == 0:
                        dve.wait_ge(s_x1, 16 * (NG - 2))
                    moments(0, n + 2)
                    moments(1, n + 3)
                    deviations(2)
                shared_low(n)
                shared_add(n, n)
                if edge and n < 2:
                    expert_weights(n)
                if edge and n == NG - 2:
                    expert_weights(2)

            f_state[0] = 0
            moments(0, 0)
            moments(1, 1)
            deviations(2)
            pairs(dve, 0, NG, first_ffn)
            tables(0)
            phase_end(dve, 1)
            experts(0)
            phase_end(dve, 2)

            def streams(m, u, route, attending, ready):
                n = m + NG
                if route:
                    moments(0, m)
                if ready:
                    dve.wait_ge(s_comb, m + 3)
                    moments(1, m + 2)
                deviations(1)
                if attending:
                    attend(m + 1, 0, 1)
                    attend(m + 1, 1, 0)
                if route:
                    choose(n, u, m)
                if attending:
                    attend(m + 1, 1, 1)
                    divide(m + 1)
                if ready:
                    features(m + 2, 0)
                    features(m + 2, 1)
                if route:
                    place(n, u, m)
                if attending:
                    y_low(m + 1)
                if route:
                    for c in range(SC):
                        for h in range(2):
                            shared(n, c, h)
                if attending:
                    attention_add(m + 1)
                if route:
                    shared_low(n)
                if ready:
                    attend(m + 2, 0, 0)
                if route:
                    shared_add(n, m)

            f_state[0] = 1
            for u in range(2):
                dve.tensor_scalar(row[u][:, :, WORDS - 2], row[u][:, :, WORDS - 2], float(-T), None, ALU.add)
            streams_of(dve, streams)
            tables(1)
            phase_end(dve, 3)
            experts(1)
            phase_end(dve, 4)
            pairs(dve, NG, 2 * NG, lambda n, u: combine(n, u, n - NG))


_INS = ['L0_attn_x', 'L0_attn_W_attn', 'L0_attn_b_attn', 'L0_attn_W_proj', 'L0_attn_b_proj', 'L0_ffn_gate_w',
        'L0_ffn_Wg', 'L0_ffn_Wu', 'L0_ffn_Wd', 'L0_ffn_Sg', 'L0_ffn_Su', 'L0_ffn_Sd']


def kernel(**inputs):
    import numpy as _np
    import concourse.bacc as _bacc
    from concourse import mybir as _mybir
    from concourse.bass_utils import run_bass_kernel_spmd as _run

    nc = _bacc.Bacc("TRN2", target_bir_lowering=False, num_devices=1)
    arrays, args = {}, []
    for name in _INS:
        a = _np.ascontiguousarray(inputs[name])
        if name == 'L0_attn_x':
            a = a.reshape(T, D)
        arrays[f"in_{name}_dram"] = a
        args.append(nc.dram_tensor(f"in_{name}_dram", a.shape, _mybir.dt.from_np(a.dtype), kind="ExternalInput").ap())
    args.append(nc.dram_tensor("out_0_dram", (T, D), _mybir.dt.float32, kind="ExternalOutput").ap())
    macaron(nc, *args)
    r = _run(nc, [arrays], core_ids=[0])
    return r.results[0]["out_0_dram"].reshape(B, S, D)
```

```python
from contextlib import ExitStack

import concourse.bass as bass
from concourse import mybir

F32, F16, I32, U32 = mybir.dt.float32, mybir.dt.float16, mybir.dt.int32, mybir.dt.uint32
ALU = mybir.AluOpType
ACT = mybir.ActivationFunctionType
AX = mybir.AxisListType

P = 128
D = 128
E = 8
K = 2
FI = 352
FS = 176
B, S = 32, 256
T = B * S
TILE = P
NJ = 4
GT = NJ * TILE
NG = T // GT
HEADS, HD = 16, 8
BLK = 256
HALVES = BLK // P
NBLK = T * K // BLK + E
NC = 3
FP = NC * P
SC = 2
UNITS = SC * 2
SW = FS // SC
REGION = T + BLK
ROWS = E * REGION + E * BLK
WORDS = 130
NOTOK = float(1 << 20)

SX, SWT, SH, SY, SBIAS = 10, 8, 2, 4, 10
EPS_LN, EPS_DEN = 1e-5, 1e-6
VD = HD + 1
KVW = HEADS * HD * VD
ENGINES = 5
LAST = 4


def macaron(nc, x, w_attn, b_attn, w_proj, b_proj, gate_w, wg, wu, wd, sg, su, sd, out):
    ctx = ExitStack()
    with ctx:
        def sb(name, shape, dt=F32):
            return ctx.enter_context(nc.sbuf_tensor(name, shape, dt))

        def ps(name, shape, dt=F32):
            return ctx.enter_context(nc.psum_tensor(name, shape, dt))

        def sem(name):
            return ctx.enter_context(nc.semaphore(name))

        routed = nc.dram_tensor("routed_rows", (ROWS, WORDS), F32).ap()
        result = nc.dram_tensor("expert_results", (K * T, D), F32).ap()

        X = sb("X", [P, T // P * D])
        PR = sb("PR", [P, NG * NJ * K])
        WG = sb("WG", [P, 2, E * FP], F16)
        WU = sb("WU", [P, 2, E * FP], F16)
        WD = sb("WD", [P, 2, E * NC * D], F16)
        GW = sb("GW", [P, 2, E], F16)
        SGW = sb("SGW", [P, 2, FS], F16)
        SUW = sb("SUW", [P, 2, FS], F16)
        SDW = sb("SDW", [P, 2, SC * D], F16)
        AW = sb("AW", [P, 2, 3 * D], F16)
        PW = sb("PW", [P, 2, D], F16)
        WSIZE = E * NC * D
        space = sb("space", [P, 3 * WSIZE])
        expert_w = [space[:, w * WSIZE:(w + 1) * WSIZE] for w in range(3)]
        taken = [0]

        def reused(pattern, **sizes):
            n, at = 1, taken[0]
            for size in sizes.values():
                n *= size
            taken[0] += n
            return space[:, at:at + n].rearrange(pattern, **sizes)

        small_w = sb("small_w", [P, 2 * FS + SC * D + 4 * D + E])
        bias_f = sb("bias_f", [P, 4 * D])
        bias_l = sb("bias_l", [P, 4 * D], F16)
        bias = sb("bias", [P, 4 * D], F16)
        rows_a = sb("rows_a", [P, P], F16)
        rows_p = sb("rows_p", [P, P], F16)
        ident = sb("ident", [P, P], F16)
        before = sb("before", [P, P], F16)
        ones16 = sb("ones16", [P, P], F16)
        upto = sb("upto", [P, P])
        ones32 = sb("ones32", [P, P])
        expert_no = sb("expert_no", [P, NJ, E])
        block_no = sb("block_no", [P, NBLK])
        base = sb("base", [P, E])
        base_i = sb("base_i", [P, E], I32)
        region0 = sb("region0", [P, E])
        pad_rows = sb("pad_rows", [P, HALVES, WORDS])
        xn = sb("xn", [P, 2, NJ, D])
        stats = sb("stats", [P, 2, NJ, 6])
        mv = sb("mv", [P, 2, NJ, 2])
        var = sb("var", [P, 2, NJ])
        rstd = sb("rstd", [P, 2, NJ])
        shift = sb("shift", [P, 2, NJ])
        newton = sb("newton", [P, 2, NJ])
        row = [sb(f"row{u}", [P, NJ, WORDS]) for u in range(2)]
        xT = [sb(f"xT{u}", [P, 2, GT], F16) for u in range(2)]
        lg = sb("lg", [P, NJ, E])
        top = sb("top", [P, NJ, E])
        which = sb("which", [P, NJ, E], U32)
        margin = sb("margin", [P, NJ])
        pick = sb("pick", [P, K, NJ, E])
        chosen = sb("chosen", [P, NJ, E], F16)
        posb = sb("posb", [P, NJ, E])
        pk = sb("pk", [P, K, NJ, E])
        th = sb("th", [P, NJ])
        dstf = [sb(f"dstf{u}", [P, K, NJ]) for u in range(2)]
        dstc = sb("dstc", [P, K, NJ])
        idx = [sb(f"idx{u}", [P, K, NJ], U32) for u in range(2)]
        ssil = sb("ssil", [SW, SC, GT])
        sh32 = sb("sh32", [SW, SC, GT])
        shT = sb("shT", [SW, 2, SC, GT], F16)
        nb = sb("nb", [P, E])
        nbi = sb("nbi", [P, E], I32)
        cum = sb("cum", [P, E])
        past = sb("past", [P, NBLK, E])
        eb = sb("eb", [P, NBLK])
        startb = sb("startb", [P, NBLK])
        rowf = sb("rowf", [P, NBLK])
        row_i = sb("row_i", [P, NBLK], I32)
        exp_i = sb("exp_i", [P, NBLK], I32)
        xe = [sb(f"xe{u}", [P, HALVES, WORDS]) for u in range(2)]
        eT = [sb(f"eT{u}", [P, 2, BLK], F16) for u in range(2)]
        esil = [sb(f"esil{u}", [P, NC * BLK]) for u in range(2)]
        eh32 = [sb(f"eh32{u}", [P, NC * BLK]) for u in range(2)]
        ehT = [sb(f"ehT{u}", [P, 2, NC, BLK], F16) for u in range(2)]
        ey = [sb(f"ey{u}", [P, HALVES, D]) for u in range(2)]
        second = sb("second", [P, 2, HALVES])
        places = sb("places", [P, NBLK * HALVES])
        eidx = [sb(f"eidx{u}", [P, HALVES], U32) for u in range(2)]
        carrier = sb("carrier", [P, 2])
        Y = [reused("p (k j d) -> p k j d", k=K, j=NJ, d=D) for u in range(2)]
        YL = [space[:, u * K * GT:(u + 1) * K * GT].rearrange("p (k j d) -> p k j d", k=K, j=NJ) for u in range(LAST)]
        xa = sb("xa", [P, 2, NJ, D], F16)
        xaT = sb("xaT", [P, 2, GT], F16)
        relu = reused("p (q a d) -> p q a d", q=2, a=2, d=2 * D)
        expo = sb("expo", [P, 2, 2, 2 * D])
        qk = sb("qk", [P, 2, 2, 2 * D])
        val = sb("val", [P, 2, 2, HEADS, VD])
        kv = reused("p (q a w) -> p q a w", q=2, a=2, w=KVW)
        prod = sb("prod", [P, 2, KVW])
        num = reused("p (j h v) -> p j h v", j=NJ, h=HEADS, v=VD)
        rden = sb("rden", [P, NJ, HEADS])
        y32 = reused("p (j d) -> p j d", j=NJ, d=D)
        ya = sb("ya", [P, 2, NJ, D], F16)
        yaT = sb("yaT", [P, 2, GT], F16)

        is_row = sb("is_row", [P, 2])
        ffn = [0]

        PSUM = ps("PSUM", [P, 8 * 512])

        def bank(n, m=1):
            return PSUM[:, 512 * n:512 * (n + m)]

        PT = bank(0).bitcast(F16)
        PL = bank(1)
        PG = [bank(2), bank(3)]
        PO = bank(4)
        KV0 = (3 * 512 - KVW) // 2
        PKV = bank(5, 3)[:, KV0:KV0 + KVW]
        PE_T = bank(7).bitcast(F16)
        PE_Y = bank(6)

        s_small_weights, s_first_tokens, s_tokens = sem("s_small_weights"), sem("s_first_tokens"), sem("s_tokens")
        s_filled, s_constants, s_weights_low, s_weights_high = sem("s_filled"), sem("s_constants"), sem("s_weights_low"), sem("s_weights_high")
        s_expert_weights, s_bias_zeroed = [sem(f"s_expert_weights{w}") for w in range(3)], sem("s_bias_zeroed")
        s_phase = sem("s_phase")
        s_norm_high, s_norm_low, s_norm_turned, s_xT = sem("s_norm_high"), sem("s_norm_low"), sem("s_norm_turned"), sem("s_xT")
        s_logits, s_chosen, s_positions, s_placed_rows = sem("s_logits"), sem("s_chosen"), sem("s_positions"), sem("s_placed_rows")
        s_margin, s_tanh = sem("s_margin"), sem("s_tanh")
        s_shared_products, s_shared_silu, s_shared_hidden, s_shared_high, s_shared_low, s_shared_out, s_shared_added = (
            sem("s_shared_products"), sem("s_shared_silu"), sem("s_shared_hidden"), sem("s_shared_high"), sem("s_shared_low"), sem("s_shared_out"), sem("s_shared_added"))
        s_scattered = [sem("s_scattered0"), sem("s_scattered1")]
        s_row_ends, s_padded = sem("s_row_ends"), sem("s_padded")
        s_block_rows = [sem("s_block_rows0"), sem("s_block_rows1")]
        s_block_turned, s_block_T, s_block_products, s_block_silu, s_block_hidden, s_block_high, s_block_low, s_block_out, s_block_results, s_block_places = (
            sem("s_block_turned"), sem("s_block_T"), sem("s_block_products"), sem("s_block_silu"), sem("s_block_hidden"), sem("s_block_high"), sem("s_block_low"),
            sem("s_block_out"), sem("s_block_results"), sem("s_block_places"))
        s_carrier = sem("s_carrier")
        s_results = [sem("s_results0"), sem("s_results1")]
        s_Y = [sem("s_Y0"), sem("s_Y1")]
        s_YL = [sem(f"s_YL{u}") for u in range(LAST)]
        s_combined, s_weighed, s_deviations = sem("s_combined"), sem("s_weighed"), sem("s_deviations")
        s_attn_high, s_attn_low, s_attn_turned, s_xaT = sem("s_attn_high"), sem("s_attn_low"), sem("s_attn_turned"), sem("s_xaT")
        s_qkv_products, s_qkv_parts, s_features, s_outer, s_running_sums, s_sums_read = (
            sem("s_qkv_products"), sem("s_qkv_parts"), sem("s_features"), sem("s_outer"), sem("s_running_sums"), sem("s_sums_read"))
        s_y, s_y_high, s_y_low, s_y_turned, s_yaT, s_projected, s_attention_added = (
            sem("s_y"), sem("s_y_high"), sem("s_y_low"), sem("s_y_turned"), sem("s_yaT"), sem("s_projected"), sem("s_attention_added"))
        s_stored = sem("s_stored")

        def wait(eng, s, v):
            if not isinstance(v, int) or v > 0:
                eng.wait_ge(s, v)

        def phase_end(eng, n):
            eng.drain().then_inc(s_phase, 1)
            eng.wait_ge(s_phase, ENGINES * n)

        def pairs(eng, first, last, step, tail=2):
            step(first, 0)
            step(first + 1, 1)
            with eng.Fori(0, (last - first - 2 - tail) // 2) as i:
                step(i * 2 + (first + 2), 0)
                step(i * 2 + (first + 3), 1)
            for n in range(last - tail, last):
                step(n, n % 2)

        def streams_of(eng, step):
            step(-2, 0, False, False, True, False)
            step(-1, 1, False, True, True, False)
            step(0, 0, True, True, True, False)
            with eng.Fori(0, (NG - 4) // 2) as i:
                step(i * 2 + 1, 1, True, True, True, True)
                step(i * 2 + 2, 0, True, True, True, True)
            step(NG - 3, 1, True, True, True, True)
            step(NG - 2, 0, True, True, False, True)
            step(NG - 1, 1, True, False, False, True)
            step(NG, 0, False, False, False, True)

        def slot(n, u):
            return u if ffn[0] == 0 else 0

        def cols(n, width, at=0, size=None):
            return bass.ds(n * width + at, width if size is None else size)

        def X3(n):
            return X[:, cols(n, GT)].rearrange("p (j d) -> p j d", j=NJ)

        block = ctx.enter_context(nc.Block())

        @block.sync
        def _(sp):
            def tokens(ap, g):
                return ap[g * GT:(g + 1) * GT, :].rearrange("(j p) d -> p j d", p=P)

            sp.dma_start(X3(0), tokens(x, 0)).then_inc(s_first_tokens, 16)
            sp.dma_start(X3(1), tokens(x, 1)).then_inc(s_first_tokens, 16)
            o = 0
            for w, n in ((gate_w, E), (sg, FS), (su, FS), (w_attn, 3 * D), (w_proj, D)):
                sp.dma_start(small_w[:, o:o + n], w).then_inc(s_small_weights, 16)
                o += n
            for c in range(SC):
                sp.dma_start(small_w[0:SW, o:o + D], sd[c * SW:(c + 1) * SW, :]).then_inc(s_small_weights, 16)
                o += D
            sp.wait_ge(s_bias_zeroed, 1)
            for r in range(2):
                sp.dma_start(bias_f[r:r + 1, 0:3 * D], b_attn.rearrange("(a n) -> a n", a=1)).then_inc(s_small_weights, 16)
                sp.dma_start(bias_f[r:r + 1, 3 * D:4 * D], b_proj.rearrange("(a n) -> a n", a=1)).then_inc(s_small_weights, 16)
            for g in range(2, NG):
                sp.dma_start(X3(g), tokens(x, g)).then_inc(s_tokens, 16)
            for n, w in enumerate((wg, wu)):
                sp.dma_start(expert_w[n][:, 0:E * FI].rearrange("p (e i) -> p e i", e=E),
                             w.rearrange("e h i -> h e i")).then_inc(s_expert_weights[n], 16)
            v = expert_w[2][:, :].rearrange("p (e c h) -> p e c h", e=E, c=NC)
            for c in range(NC):
                k = min(P, FI - c * P)
                sp.dma_start(v[0:k, :, c, :], wd[:, c * P:c * P + k, :].rearrange("e k h -> k e h")
                             ).then_inc(s_expert_weights[2], 16)

            def pads(f):
                wait(sp, s_row_ends, f + 1)
                ends = nc.values_load_multi_w_load_instructions(base_i[0:1, :], engines=[sp.engine], min_val=0,
                                                                max_val=(E - 1) * REGION + T,
                                                                skip_runtime_bounds_check_because="counts of tokens")[1]
                for at in ends:
                    sp.dma_start(routed[bass.ds(at, BLK), :].rearrange("(h p) w -> p h w", p=P),
                                 pad_rows[:, :, :]).then_inc(s_padded, 16)
                sp.wait_ge(s_padded, 16 * (E * (f + 2)))

            def load_block(f):
                def step(n, u):
                    m = n - f * NBLK
                    wait(sp, s_block_T, n - 1)
                    wait(sp, s_block_places, n - 1)
                    at = sp.value_load(row_i[0:1, bass.ds(m, 1)], min_val=0, max_val=ROWS - BLK)
                    sp.dma_start(xe[u][:, :, :], routed[bass.ds(at, BLK), :].rearrange("(h p) w -> p h w", p=P)
                                 ).then_inc(s_block_rows[u], 16)
                return step

            def results(g, k):
                return result[bass.ds(g * GT + k * T, GT), :].rearrange("(j p) d -> p j d", p=P)

            def load_results(g, u):
                wait(sp, s_combined, g - 1)
                for k in range(K):
                    sp.dma_start(Y[u][:, k, :, :], results(g, k)).then_inc(s_Y[u], 16)

            def load_last(g, u):
                for k in range(K):
                    sp.dma_start(YL[u][:, k, :, :], results(g, k)).then_inc(s_YL[u], 16)

            sp.wait_ge(s_filled, 1)
            for e in range(E):
                sp.dma_start(routed[E * REGION + e * BLK:E * REGION + (e + 1) * BLK, :].rearrange("(h p) w -> p h w", p=P),
                             pad_rows[:, :, :]).then_inc(s_padded, 16)
            for f in range(2):
                pads(f)
                phase_end(sp, 2 * f + 1)
                pairs(sp, f * NBLK, (f + 1) * NBLK, load_block(f))
                phase_end(sp, 2 * f + 2)
                if f == 0:
                    pairs(sp, 0, NG, load_results)

            def store(g):
                sp.wait_ge(s_combined, g + (NG + 1))
                sp.dma_start(out[bass.ds(g * GT, GT), :].rearrange("(j p) d -> p j d", p=P), X3(g)).then_inc(s_stored, 16)

            for u in range(LAST):
                load_last(u, u)
            with sp.Fori(0, NG // LAST - 1) as i:
                for u in range(LAST):
                    store(i * LAST + u)
                    load_last(i * LAST + (LAST + u), u)
            for u in range(LAST):
                store(NG - LAST + u)
            sp.wait_ge(s_stored, 16 * NG)

        @block.gpsimd
        def _(pool):
            pool.memset(bias_f[:, :], 0.0)
            pool.drain().then_inc(s_bias_zeroed, 1)
            pool.memset(ones16[:, :], 1.0)
            pool.memset(rows_a[:, :], 0.0)
            pool.memset(rows_p[:, :], 0.0)
            pool.memset(ones32[:, :], 1.0)
            pool.memset(ident[:, :], 0.0)
            pool.memset(is_row[:, :], 0.0)
            pool.memset(pad_rows[:, :, :], 0.0)
            pool.drain()
            pool.memset(pad_rows[:, :, WORDS - 2:WORDS - 1], NOTOK)
            pool.memset(rows_a[0:2, :], 2.0 ** (SX + SWT - SBIAS))
            pool.memset(rows_p[0:2, :], 2.0 ** (SY + SWT - SBIAS))
            pool.drain().then_inc(s_filled, 1)
            pool.affine_select(out=ident[:, :], in_=ident[:, :], compare_op=ALU.not_equal, fill=1.0, base=0,
                               pattern=[[-1, P]], channel_multiplier=1)
            pool.affine_select(out=before[:, :], in_=ones16[:, :], compare_op=ALU.is_gt, fill=0.0, base=0,
                               pattern=[[1, P]], channel_multiplier=-1)
            pool.affine_select(out=upto[:, :], in_=ones32[:, :], compare_op=ALU.is_ge, fill=0.0, base=0,
                               pattern=[[1, P]], channel_multiplier=-1)
            pool.affine_select(out=is_row[:, :], in_=is_row[:, :], compare_op=ALU.not_equal, fill=1.0, base=0,
                               pattern=[[-1, 2]], channel_multiplier=1)
            pool.iota(expert_no[:, :, :], [[0, NJ], [1, E]], base=0, channel_multiplier=0,
                      allow_small_or_imprecise_dtypes=True)
            pool.iota(block_no[:, :], [[1, NBLK]], base=0, channel_multiplier=0,
                      allow_small_or_imprecise_dtypes=True)
            pool.iota(region0[:, :], [[REGION, E]], base=0, channel_multiplier=0,
                      allow_small_or_imprecise_dtypes=True)
            for u in range(2):
                pool.iota(row[u][:, :, WORDS - 2], [[TILE, NJ]], base=u * GT, channel_multiplier=1,
                          allow_small_or_imprecise_dtypes=True)
            pool.drain().then_inc(s_constants, 1)

            def scatter(n, u):
                pool.wait_ge(s_placed_rows, n + 1)
                pool.tensor_tensor(dstc[:, :, :], dstf[u][:, :, :],
                                   ones32[:, 0:K * NJ].rearrange("p (k j) -> p k j", k=K), ALU.mult)
                pool.drain()
                pool.tensor_copy(idx[u][:, :, :], dstc[:, :, :])
                pool.drain()
                for k in range(K):
                    for j in range(NJ):
                        pool.indirect_dma_start(routed, bass.IndirectOffsetOnAxis(ap=idx[u][:, k, j:j + 1], axis=0),
                                                row[u][:, j, :], None).then_inc(s_scattered[u], 16)

            def results(n, u):
                pool.wait_ge(s_block_results, n + 1)
                pool.tensor_tensor(carrier[:, u:u + 1], ones32[:, 0:1], ones32[:, 0:1], ALU.mult).then_inc(s_carrier, 1)
                for h in range(HALVES):
                    pool.indirect_dma_start(result, bass.IndirectOffsetOnAxis(ap=eidx[u][:, h:h + 1], axis=0),
                                            ey[u][:, h, :], None, bounds_check=K * T - 1, oob_is_err=False
                                            ).then_inc(s_results[u], 16)

            def low(n, dst, slot, high, s_high, s_low):
                pool.wait_ge(s_high, n + 1)
                pool.tensor_tensor(dst, xn[:, slot, :, :], high, ALU.subtract).then_inc(s_low, 1)

            def outer(m, q, a):
                pool.wait_ge(s_features, m * 2 + (q + 1))
                k4 = qk[:, q, a, D:2 * D].rearrange("p (h i j) -> p h i j", h=HEADS, j=1).to_broadcast([P, HEADS, HD, VD])
                v4 = val[:, q, a, :, :].rearrange("p h (i j) -> p h i j", i=1).to_broadcast([P, HEADS, HD, VD])
                pool.tensor_tensor(kv[:, q, a, :].rearrange("p (h i j) -> p h i j", h=HEADS, i=HD), k4, v4, ALU.mult
                                   ).then_inc(s_outer, 1)

            def combine(g, u):
                pool.wait_ge(s_weighed, g - 1)
                for k in range(K):
                    pool.tensor_tensor(X3(g), X3(g), Y[u][:, k, :, :], ALU.add)
                    last = pool.drain()
                last.then_inc(s_combined, 1)

            def row_low(n, u):
                low(n, row[u][:, :, D // 2:D].bitcast(F16), slot(n, u), row[u][:, :, 0:D // 2].bitcast(F16), s_norm_high, s_norm_low)

            for f in range(2):
                ffn[0] = f
                if f == 0:
                    pairs(pool, 0, NG, scatter)
                else:
                    def step(m, u, route, attend, ready, settle):
                        if attend:
                            outer(m + 1, 1, 0)
                        if ready and not (isinstance(m, int) and m in (-2, NG - 3)):
                            combine(m + 3, 1 - u)
                        if route:
                            row_low(m + NG, u)
                        if attend:
                            outer(m + 1, 1, 1)
                        if ready:
                            low(m + 2, xa[:, 1, :, :], 1, xa[:, 0, :, :], s_attn_high, s_attn_low)
                        if settle:
                            scatter(m + (NG - 1), 1 - u)
                        if ready:
                            outer(m + 2, 0, 0)
                            outer(m + 2, 0, 1)
                    for q in range(2):
                        pool.memset(val[:, q, :, :, HD:VD], 1.0)
                    streams_of(pool, step)
                for u in range(2):
                    pool.wait_ge(s_scattered[u], 16 * K * NJ * NG // 2 * (f + 1))
                phase_end(pool, 2 * f + 1)
                pairs(pool, f * NBLK, (f + 1) * NBLK, results)
                for u in range(2):
                    pool.wait_ge(s_results[u], 16 * HALVES * NBLK // 2 * (f + 1))
                phase_end(pool, 2 * f + 2)

        @block.scalar
        def _(act):
            def part(dst, src):
                act.activation(dst, src, ACT.Copy, scale=float(2 ** SWT))

            def expert_weights(n):
                act.wait_ge(s_expert_weights[n], 16 if n < 2 else 16 * NC)
                if n < 2:
                    W = (WG, WU)[n]
                    part(W[:, 0, :].rearrange("p (e i) -> p e i", e=E)[:, :, 0:FI],
                         expert_w[n][:, 0:E * FI].rearrange("p (e i) -> p e i", e=E))
                else:
                    v, w = (a.rearrange("p (e c h) -> p e c h", e=E, c=NC) for a in (expert_w[2][:, :], WD[:, 0, :]))
                    part(w[:, :, 0:NC - 1, :], v[:, :, 0:NC - 1, :])
                    part(w[0:FI - 2 * P, :, NC - 1, :], v[0:FI - 2 * P, :, NC - 1, :])
                act.drain().then_inc(s_weights_high, 1)

            def normalize(slot, g):
                xs = X3(g)
                for j in range(NJ):
                    act.activation(xn[:, slot, j, :], xs[:, j, :], ACT.Identity, scale=rstd[:, slot, j:j + 1],
                                   bias=shift[:, slot, j:j + 1])
                act.drain()

            def norm(n, u, g):
                act.wait_ge(s_deviations, n - u + 2 if ffn[0] == 0 else g + (NG + 3))
                normalize(slot(n, u), g)

            def high(n, u):
                wait(act, s_scattered[u], (n - u) * (16 * K * NJ // 2))
                act.activation(row[u][:, :, 0:D // 2].bitcast(F16), xn[:, slot(n, u), :, :], ACT.Copy).then_inc(s_norm_high, 1)

            def evacuate(n, u):
                act.wait_ge(s_norm_turned, n + 1)
                act.activation(xT[u][:, :, :], PT[:, :].rearrange("p (a t) -> p a t", a=2), ACT.Copy).then_inc(s_xT, 1)

            def shared_silu(n, c, h):
                act.wait_ge(s_shared_products, n * UNITS + (c * 2 + h + 1))
                act.activation(ssil[:, c, h * GT // 2:(h + 1) * GT // 2], PG[h][0:SW, 0:GT // 2], ACT.Silu,
                               scale=2.0 ** -(SX + SWT)).then_inc(s_shared_silu, 1)

            def shared_high(n):
                act.wait_ge(s_shared_hidden, n * UNITS + UNITS)
                wait(act, s_shared_out, n)
                act.activation(shT[:, 0, :, :], sh32[:, :, :], ACT.Copy).then_inc(s_shared_high, 1)

            def tanh(n):
                act.wait_ge(s_margin, n + 1)
                act.activation(th[:, :], margin[:, :], ACT.Tanh, scale=0.5 * 2.0 ** -(SX + SWT)).then_inc(s_tanh, 1)

            def norm_high(m):
                act.wait_ge(s_deviations, m + (NG + 1))
                normalize(1, m)
                act.activation(xa[:, 0, :, :], xn[:, 1, :, :], ACT.Copy).then_inc(s_attn_high, 1)

            def norm_evacuate(m):
                act.wait_ge(s_attn_turned, m + 1)
                act.activation(xaT[:, :, :], PT[:, :].rearrange("p (a t) -> p a t", a=2), ACT.Copy).then_inc(s_xaT, 1)

            def features(m, q, a):
                act.wait_ge(s_qkv_products, m * NJ + (2 * q + a + 1))
                z = PG[a]
                act.activation(relu[:, q, a, :], z[:, 0:2 * D], ACT.Relu, scale=2.0 ** -(SX + SWT))
                act.activation(expo[:, q, a, :], z[:, 0:2 * D], ACT.Exp, scale=2.0 ** -(SX + SWT))
                act.activation(val[:, q, a, :, 0:HD], z[:, 2 * D:3 * D].rearrange("p (h j) -> p h j", h=HEADS), ACT.Copy,
                               scale=2.0 ** -(SX + SWT)).then_inc(s_qkv_parts, 1)

            def weigh(g, u):
                act.wait_ge(s_Y[u], (g - u) * (16 * K // 2) + 16 * K)
                for k in range(K):
                    for j in range(NJ):
                        last = act.activation(Y[u][:, k, j, :], Y[u][:, k, j, :], ACT.Copy,
                                              scale=PR[:, cols(g, NJ * K, j * K + k, 1)])
                last.then_inc(s_weighed, 1)

            def weigh_last(g, u):
                act.wait_ge(s_YL[u], (g - u) * (16 * K // LAST) + 16 * K)
                for j in range(NJ):
                    last = act.activation(YL[u][:, 1, j, :], YL[u][:, 1, j, :], ACT.Copy,
                                          scale=PR[:, cols(g, NJ * K, j * K + 1, 1)])
                last.then_inc(s_weighed, 1)

            def y_high(m):
                act.wait_ge(s_y, m + 1)
                act.activation(ya[:, 0, :, :], y32[:, :, :], ACT.Copy, scale=float(2 ** SY)).then_inc(s_y_high, 1)

            def y_evacuate(m):
                act.wait_ge(s_y_turned, m + 1)
                act.activation(yaT[:, :, :], PT[:, :].rearrange("p (a t) -> p a t", a=2), ACT.Copy).then_inc(s_yaT, 1)

            def silu(n, u):
                act.wait_ge(s_block_products, n + 1)
                act.activation(esil[u][:, :], PSUM[:, 1536 * u:1536 * u + 768], ACT.Silu,
                               scale=2.0 ** -(SX + SWT)).then_inc(s_block_silu, 1)

            def hi(n, u):
                act.wait_ge(s_block_hidden, n + 1)
                act.activation(ehT[u][:, 0, :, :], eh32[u][:, :].rearrange("p (c t) -> p c t", c=NC), ACT.Copy
                               ).then_inc(s_block_high, 1)

            def results(n, u):
                act.wait_ge(s_block_out, n + 1)
                wait(act, s_results[u], res_value(n, u))
                wait(act, s_carrier, n - 1)
                act.activation(eidx[u][:, :], places[:, cols(n - ffn[0] * NBLK, HALVES)], ACT.Copy)
                act.activation(ey[u][:, :, :], PE_Y[:, 0:BLK].rearrange("p (h d) -> p h d", h=HALVES), ACT.Copy,
                               scale=0.5 * 2.0 ** -(SH + SWT)).then_inc(s_block_results, 1)

            def res_value(n, u):
                return (n - u) * (16 * HALVES // 2)

            def experts(f):
                n0, n1 = f * NBLK, (f + 1) * NBLK

                def step(n, u):
                    silu(n, u)
                    hi(n - 1, 1 - u)
                    results(n - 2, u)

                silu(n0, 0)
                silu(n0 + 1, 1)
                hi(n0, 0)
                step(n0 + 2, 0)
                step(n0 + 3, 1)
                with act.Fori(0, (NBLK - 4) // 2) as i:
                    step(i * 2 + (n0 + 4), 0)
                    step(i * 2 + (n0 + 5), 1)
                hi(n1 - 1, 1)
                results(n1 - 2, 0)
                results(n1 - 1, 1)

            def first_ffn(n, u):
                edge = isinstance(n, int)
                ahead = not (edge and n == NG - 1)
                if ahead:
                    norm(n + 1, 1 - u, n + 1)
                for h in range(2):
                    shared_silu(n, 0, h)
                tanh(n)
                if ahead:
                    high(n + 1, 1 - u)
                for h in range(2):
                    shared_silu(n, 1, h)
                if ahead:
                    evacuate(n + 1, 1 - u)
                shared_high(n)
                if edge and n < 2:
                    expert_weights(n)
                if edge and n == NG - 2:
                    expert_weights(2)

            def streams(m, u, route, attend, ready, settle):
                n = m + NG
                if ready and not (isinstance(m, int) and m in (-2, NG - 3)):
                    weigh(m + 3, 1 - u)
                if settle:
                    for h in range(2):
                        shared_silu(n - 1, 0, h)
                    tanh(n - 1)
                if route:
                    norm(n, u, m)
                    high(n, u)
                if ready:
                    norm_high(m + 2)
                if route:
                    evacuate(n, u)
                if settle:
                    for h in range(2):
                        shared_silu(n - 1, 1, h)
                if ready:
                    norm_evacuate(m + 2)
                if settle:
                    shared_high(n - 1)
                if ready:
                    for q in range(2):
                        for a in range(2):
                            features(m + 2, q, a)
                if attend:
                    y_high(m + 1)
                    y_evacuate(m + 1)

            ffn[0] = 0
            act.wait_ge(s_small_weights, 16 * 11)
            act.wait_ge(s_weights_low, 1)
            o = 0
            for w, n in ((GW, E), (SGW, FS), (SUW, FS), (AW, 3 * D), (PW, D)):
                part(w[:, 0, :], small_w[:, o:o + n])
                o += n
            part(SDW[0:SW, 0, :], small_w[0:SW, o:o + SC * D])
            act.activation(bias[:, :], bias_f[:, :], ACT.Copy, scale=2.0 ** SBIAS)
            act.drain().then_inc(s_weights_high, 1)

            norm(0, 0, 0)
            high(0, 0)
            evacuate(0, 0)
            pairs(act, 0, NG, first_ffn)
            phase_end(act, 1)
            experts(0)
            phase_end(act, 2)
            ffn[0] = 1
            streams_of(act, streams)
            phase_end(act, 3)
            experts(1)
            phase_end(act, 4)
            with act.Fori(0, NG // LAST) as i:
                for u in range(LAST):
                    weigh_last(i * LAST + u, u)

        @block.tensor
        def _(pe):
            def product(dst, a, b, start=True, stop=True):
                pe.matmul(dst, a[0], b[0], start=start, stop=False)
                pe.matmul(dst, a[0], b[1], start=False, stop=False)
                return pe.matmul(dst, a[1], b[0], start=False, stop=stop)

            def transpose_group(src, s):
                for part in range(2):
                    for j in range(NJ):
                        mm = pe.transpose(PT[:, part * GT + j * P:part * GT + (j + 1) * P], src(part, j), ident[:, :])
                mm.then_inc(s, 1)

            def transposes(n, u, m=None):
                pe.wait_ge(s_norm_low, n + 1)
                if m is None:
                    wait(pe, s_xT, n)
                else:
                    pe.wait_ge(s_yaT, m + 1)
                transpose_group(lambda part, j: row[u][:, j, part * D // 2:(part + 1) * D // 2].bitcast(F16), s_norm_turned)

            def logits(n, u):
                pe.wait_ge(s_xT, n + 1)
                for j in range(NJ):
                    t = slice(j * P, (j + 1) * P)
                    for a, b in ((0, 0), (0, 1), (1, 0), (1, 1)):
                        mm = pe.matmul(PL[:, j * E:(j + 1) * E], xT[u][:, a, t], GW[:, b, :], start=(a + b == 0), stop=(a + b == 2))
                mm.then_inc(s_logits, 1)

            def gate_up(n, u, c, h, last=False):
                i = c * 2 + h
                if c == 1 or ffn[0] == 0 or last:
                    wait(pe, s_shared_hidden, n * UNITS + (i - 1))
                w = slice(c * SW, (c + 1) * SW)
                t = slice(h * GT // 2, (h + 1) * GT // 2)
                xh = [xT[u][:, a, t] for a in range(2)]
                product(PG[h][0:SW, 0:GT // 2], [SGW[:, 0, w], SGW[:, 1, w]], xh)
                product(PG[h][0:SW, GT // 2:GT], [SUW[:, 0, w], SUW[:, 1, w]], xh).then_inc(s_shared_products, 1)

            def positions(n):
                pe.wait_ge(s_chosen, n + 1)
                pos = PL[:, 64:64 + (NJ + 1) * E]
                ch = chosen[:, :, :].rearrange("p j e -> p (j e)")
                pe.matmul(pos[:, 0:NJ * E], before[:, :], ch, start=True, stop=False, skip_group_check=True)
                for d in range(1, NJ + 1):
                    mm = pe.matmul(pos[:, d * E:(NJ + 1) * E], ones16[:, :], ch[:, 0:(NJ + 1 - d) * E], start=False,
                                   stop=(d == NJ), skip_group_check=True)
                mm.then_inc(s_positions, 1)

            def down(n, m=None):
                pe.wait_ge(s_shared_low, n + 1)
                if m is None:
                    wait(pe, s_shared_added, n)
                else:
                    pe.wait_ge(s_attention_added, m + 1)
                for j in range(NJ):
                    t = slice(j * P, (j + 1) * P)
                    for c in range(SC):
                        h = slice(c * D, (c + 1) * D)
                        mm = product(PO[:, j * D:(j + 1) * D], [shT[:, 0, c, t], shT[:, 1, c, t]],
                                     [SDW[0:SW, 0, h], SDW[0:SW, 1, h]], start=(c == 0), stop=(c == SC - 1))
                mm.then_inc(s_shared_out, 1)

            def attention_transposes(m):
                pe.wait_ge(s_attn_low, m + 1)
                if not isinstance(m, int) or m > 1:
                    pe.wait_ge(s_xT, m + (NG - 1))
                transpose_group(lambda part, j: xa[:, part, j, :], s_attn_turned)

            def qkv_products(m, q, a):
                j = 2 * q + a
                if q == 0:
                    pe.wait_ge(s_xaT, m + 1)
                    if not isinstance(m, int) or m > 2:
                        pe.wait_ge(s_shared_hidden, (m + (NG - 2)) * UNITS)
                    else:
                        wait(pe, s_qkv_parts, m * NJ)
                else:
                    pe.wait_ge(s_qkv_parts, m * NJ + (a + 1))
                t = slice(j * P, (j + 1) * P)
                pe.matmul(PG[a][:, 0:3 * D], rows_a[:, :], bias[:, 0:3 * D], start=True, stop=False)
                product(PG[a][:, 0:3 * D], [xaT[:, 0, t], xaT[:, 1, t]], [AW[:, 0, :], AW[:, 1, :]], start=False
                        ).then_inc(s_qkv_products, 1)

            def running_sums(m, q, a):
                j = 2 * q + a
                pe.wait_ge(s_outer, m * NJ + (j + 1))
                wait(pe, s_sums_read, m * NJ + j)
                for lo, hi in ((0, 512 - KV0), (512 - KV0, 1024 - KV0), (1024 - KV0, KVW)):
                    mm = pe.matmul(PKV[:, lo:hi], upto[:, :], kv[:, q, a, lo:hi], start=True, stop=(a == 0))
                    if a:
                        mm = pe.matmul(PKV[:, lo:hi], ones32[:, :], kv[:, q, 0, lo:hi], start=False, stop=True)
                mm.then_inc(s_running_sums, 1)

            def y_transposes(m, ready):
                pe.wait_ge(s_y_low, m + 1)
                if ready:
                    pe.wait_ge(s_xaT, m + 2)
                transpose_group(lambda part, j: ya[:, part, j, :], s_y_turned)

            def project(m):
                pe.wait_ge(s_yaT, m + 1)
                if not isinstance(m, int) or m > 1:
                    pe.wait_ge(s_shared_added, m + (NG - 1))
                for j in range(NJ):
                    t = slice(j * P, (j + 1) * P)
                    pe.matmul(PO[:, j * D:(j + 1) * D], rows_p[:, :], bias[:, 3 * D:4 * D], start=True, stop=False)
                    mm = product(PO[:, j * D:(j + 1) * D], [yaT[:, 0, t], yaT[:, 1, t]], [PW[:, 0, :], PW[:, 1, :]],
                                 start=False)
                mm.then_inc(s_projected, 1)

            def block_transposes(n, u):
                pe.wait_ge(s_block_rows[u], (n - u) * 8 + 16)
                wait(pe, s_block_T, n)
                for part in range(2):
                    for h in range(HALVES):
                        at = part * BLK + h * P
                        mm = pe.transpose(PE_T[:, at:at + P],
                                          xe[u][:, h, part * D // 2:(part + 1) * D // 2].bitcast(F16), ident[:, :])
                mm.then_inc(s_block_turned, 1)

            def experts_of(m, count):
                return nc.values_load_multi_w_load_instructions(exp_i[0:1, bass.ds(m, count)], engines=[pe.engine],
                                                                min_val=0, max_val=E - 1,
                                                                skip_runtime_bounds_check_because="tables() clamps them")[1]

            def block_gate_up(n, u, e):
                pe.wait_ge(s_block_T, n + 1)
                wait(pe, s_block_hidden, n - 1)
                for W, o in ((WG, 0), (WU, NC * BLK)):
                    for c in range(NC):
                        w = [W[:, a, bass.ds(e * FP + c * P, P)] for a in range(2)]
                        at = 1536 * u + o + c * BLK
                        mm = product(PSUM[:, at:at + BLK], w, [eT[u][:, 0, :], eT[u][:, 1, :]])
                mm.then_inc(s_block_products, 1)

            def block_down(n, u, e):
                pe.wait_ge(s_block_low, n + 1)
                wait(pe, s_block_results, n)
                for h in range(HALVES):
                    t = slice(h * P, (h + 1) * P)
                    for c in range(NC):
                        w = [WD[:, a, bass.ds(e * (NC * D) + c * D, D)] for a in range(2)]
                        mm = product(PE_Y[:, h * D:(h + 1) * D], [ehT[u][:, 0, c, t], ehT[u][:, 1, c, t]], w,
                                     start=(c == 0), stop=(c == NC - 1))
                mm.then_inc(s_block_out, 1)

            def experts(f):
                n0, n1 = f * NBLK, (f + 1) * NBLK

                def step(n, u, e, e_down=None, ahead=True):
                    if ahead:
                        block_transposes(n + 1, 1 - u)
                    block_gate_up(n, u, e)
                    if e_down is not None:
                        block_down(n - 2, u, e_down)

                e = experts_of(0, 2)
                block_transposes(n0, 0)
                step(n0, 0, e[0])
                step(n0 + 1, 1, e[1])
                with pe.Fori(0, (NBLK - 4) // 4) as i:
                    e = experts_of(i * 4, 6)
                    for b in range(4):
                        step(i * 4 + (n0 + 2 + b), b % 2, e[b + 2], e[b])
                e = experts_of(NBLK - 4, 4)
                step(n1 - 2, 0, e[2], e[0])
                step(n1 - 1, 1, e[3], e[1], ahead=False)
                block_down(n1 - 2, 0, e[2])
                block_down(n1 - 1, 1, e[3])

            def keep_warm(count):
                for _ in range(count):
                    pe.matmul(bank(0)[:, 0:3 * D], ident[:, :], AW[:, 0, :], start=True, stop=True)

            pe.wait_ge(s_constants, 1)
            pe.wait_ge(s_weights_low, 2)

            def first_ffn(n, u):
                positions(n)
                if not isinstance(n, int) or n > 0:
                    down(n - 1)
                for h in range(2):
                    gate_up(n, u, 1, h)
                if not isinstance(n, int) or n < NG - 1:
                    transposes(n + 1, 1 - u)
                    logits(n + 1, 1 - u)
                    for h in range(2):
                        gate_up(n + 1, 1 - u, 0, h)
                    keep_warm(6)

            def streams(m, u, route, attend, ready, settle):
                n = m + NG
                if attend:
                    running_sums(m + 1, 0, 1)
                if settle:
                    last = isinstance(m, int) and m >= NG - 1
                    if not last:
                        pe.wait_ge(s_qkv_parts, (m + 1) * NJ + NJ)
                    for h in range(2):
                        gate_up(n - 1, 1 - u, 0, h, last=last)
                if attend:
                    keep_warm(8)
                    running_sums(m + 1, 1, 0)
                if settle:
                    for h in range(2):
                        gate_up(n - 1, 1 - u, 1, h)
                if route:
                    transposes(n, u, m)
                    if settle:
                        pe.wait_ge(s_placed_rows, n)
                    logits(n, u)
                if ready:
                    attention_transposes(m + 2)
                if attend:
                    running_sums(m + 1, 1, 1)
                if route:
                    positions(n)
                if ready:
                    for q in range(2):
                        for a in range(2):
                            qkv_products(m + 2, q, a)
                if settle:
                    if isinstance(m, int) and m == NG:
                        pe.wait_ge(s_shared_added, n - 1)
                        down(n - 1, m - 1)
                    else:
                        down(n - 1, m)
                if attend:
                    y_transposes(m + 1, ready)
                if ready:
                    running_sums(m + 2, 0, 0)
                if attend:
                    project(m + 1)

            ffn[0] = 0
            transposes(0, 0)
            logits(0, 0)
            for h in range(2):
                gate_up(0, 0, 0, h)
            pairs(pe, 0, NG, first_ffn)
            down(NG - 1)
            phase_end(pe, 1)
            experts(0)
            phase_end(pe, 2)
            ffn[0] = 1
            streams_of(pe, streams)
            phase_end(pe, 3)
            experts(1)
            phase_end(pe, 4)

        @block.vector
        def _(dve):
            def low(dst, src, high, scale):
                return dve.scalar_tensor_tensor(out=dst, in0=src, scalar=float(2 ** scale), in1=high,
                                                op0=ALU.mult, op1=ALU.subtract)

            def e3(ap, n):
                return ap.rearrange("p (e i) -> p e i", e=E)[:, :, 0:n]

            for W in (WG, WU):
                dve.memset(W[:, :, :].rearrange("p a (e i) -> p (a e) i", e=E)[:, :, FI:FP], 0.0)
            for a in range(2):
                dve.memset(WD[FI - 2 * P:P, a, :].rearrange("p (e c h) -> p e c h", e=E, c=NC)[:, :, NC - 1, :], 0.0)
            dve.drain().then_inc(s_weights_low, 1)

            def expert_weights(n):
                dve.wait_ge(s_weights_high, n + 2)
                if n < 2:
                    W = (WG, WU)[n]
                    low(e3(W[:, 1, :], FI), expert_w[n][:, 0:E * FI].rearrange("p (e i) -> p e i", e=E), e3(W[:, 0, :], FI), SWT)
                else:
                    v, h, l = (a.rearrange("p (e c h) -> p e c h", e=E, c=NC) for a in (expert_w[2][:, :], WD[:, 0, :], WD[:, 1, :]))
                    low(l[:, :, 0:NC - 1, :], v[:, :, 0:NC - 1, :], h[:, :, 0:NC - 1, :], SWT)
                    q = FI - 2 * P
                    low(l[0:q, :, NC - 1, :], v[0:q, :, NC - 1, :], h[0:q, :, NC - 1, :], SWT)

            def moments(slot, g):
                xs = X3(g)
                for j in range(NJ):
                    dve.bn_stats(stats[:, slot, j, :], xs[:, j, :])
                dve.drain()
                for j in range(NJ):
                    dve.bn_aggr(mv[:, slot, j, :], stats[:, slot, j, :])

            def deviations(count):
                v, y, a = var[:, :, :], rstd[:, :, :], newton[:, :, :]
                dve.drain()
                dve.tensor_scalar(v, mv[:, :, :, 1], EPS_LN, 2.0 ** (-2 * SX), ALU.add, ALU.mult)
                dve.drain()
                dve.tensor_single_scalar(a.bitcast(I32), v.bitcast(I32), 1, ALU.arith_shift_right)
                dve.drain()
                dve.tensor_scalar(y.bitcast(I32), a.bitcast(I32), -1.0, float(0x5f3759df), ALU.mult, ALU.add)
                dve.drain()
                for _ in range(3):
                    dve.tensor_tensor(a, y, y, ALU.mult)
                    dve.drain()
                    dve.scalar_tensor_tensor(out=a, in0=a, scalar=-0.5, in1=v, op0=ALU.mult, op1=ALU.mult)
                    dve.drain()
                    dve.scalar_tensor_tensor(out=y, in0=a, scalar=1.5, in1=y, op0=ALU.add, op1=ALU.mult)
                    dve.drain()
                dve.scalar_tensor_tensor(out=shift[:, :, :], in0=mv[:, :, :, 0], scalar=-1.0, in1=y, op0=ALU.mult,
                                         op1=ALU.mult).then_inc(s_deviations, count)

            def choose(n, u, g):
                dve.wait_ge(s_logits, n + 1)
                dve.tensor_copy(lg[:, :, :], PL[:, 0:NJ * E].rearrange("p (j e) -> p j e", j=NJ))
                dve.drain()
                for j in range(NJ):
                    dve.max(top[:, j, :], lg[:, j, :])
                dve.drain()
                for j in range(NJ):
                    dve.max_index(which[:, j, :], top[:, j, :], lg[:, j, :])
                dve.tensor_tensor(margin[:, :], top[:, :, 0], top[:, :, 1], ALU.subtract).then_inc(s_margin, 1)
                dve.drain()
                dve.tensor_tensor(pick[:, :, :, :],
                                  expert_no[:, :, :].rearrange("p (k j) e -> p k j e", k=1).to_broadcast([P, K, NJ, E]),
                                  which[:, :, 0:K].rearrange("p j (k e) -> p k j e", e=1).to_broadcast([P, K, NJ, E]),
                                  ALU.is_equal)
                dve.tensor_copy(row[u][:, :, WORDS - 1], which[:, :, 0])
                if not isinstance(n, int) or n >= 2:
                    dve.tensor_scalar(row[u][:, :, WORDS - 2], row[u][:, :, WORDS - 2], float(2 * GT), None, ALU.add)
                dve.drain()
                dve.tensor_tensor(chosen[:, :, :], pick[:, 0, :, :], pick[:, 1, :, :], ALU.add).then_inc(s_chosen, 1)

            def place(n, u, g):
                dve.wait_ge(s_positions, n + 1)
                pos = PL[:, 64:64 + (NJ + 1) * E].rearrange("p (j e) -> p j e", j=NJ + 1)
                bj = base[:, :].rearrange("p (j e) -> p j e", j=1).to_broadcast([P, NJ, E])
                dve.tensor_tensor(posb[:, :, :], pos[:, 0:NJ, :], bj, ALU.add)
                dve.drain()
                dve.tensor_tensor(base[:, :], base[:, :], pos[:, NJ, :], ALU.add)
                pb = posb[:, :, :].rearrange("p (k j) e -> p k j e", k=1).to_broadcast([P, K, NJ, E])
                dve.tensor_tensor(pk[:, :, :, :], pick[:, :, :, :], pb, ALU.mult)
                dve.drain()
                dve.tensor_reduce(dstf[u][:, :, :], pk[:, :, :, :], AX.X, ALU.add).then_inc(s_placed_rows, 1)

            def probabilities(n, g):
                dve.wait_ge(s_tanh, n + 1)
                pr = PR[:, cols(g, NJ * K)].rearrange("p (j k) -> p j k", k=K)
                for k in range(K):
                    dve.tensor_scalar(pr[:, :, k], th[:, :], 0.5 - k, 0.5, ALU.mult, ALU.add)

            def shared(n, c, h):
                dve.wait_ge(s_shared_silu, n * UNITS + (c * 2 + h + 1))
                t = slice(h * GT // 2, (h + 1) * GT // 2)
                dve.scalar_tensor_tensor(out=sh32[:, c, t], in0=PG[h][0:SW, GT // 2:GT], scalar=2.0 ** (SH - SX - SWT),
                                         in1=ssil[:, c, t], op0=ALU.mult, op1=ALU.mult).then_inc(s_shared_hidden, 1)

            def shared_low(n):
                dve.wait_ge(s_shared_high, n + 1)
                low(shT[:, 1, :, :], sh32[:, :, :], shT[:, 0, :, :], 0).then_inc(s_shared_low, 1)

            def shared_add(n, g):
                dve.wait_ge(s_shared_out, n + 1)
                xg = X[:, cols(g, GT)]
                dve.scalar_tensor_tensor(out=xg, in0=PO[:, :], scalar=0.5 * 2.0 ** -(SH + SWT), in1=xg,
                                         op0=ALU.mult, op1=ALU.add).then_inc(s_shared_added, 1)

            def ends():
                dve.drain()
                dve.tensor_copy(base_i[:, :], base[:, :]).then_inc(s_row_ends, 1)

            def tables():
                dve.tensor_tensor(nb[:, :], base[:, :], region0[:, :], ALU.subtract)
                dve.drain()
                dve.tensor_scalar(nb[:, :], nb[:, :], float(BLK - 1), None, ALU.add)
                dve.drain()
                dve.tensor_copy(nbi[:, :], nb[:, :])
                dve.drain()
                dve.tensor_single_scalar(nbi[:, :], nbi[:, :], BLK.bit_length() - 1, ALU.arith_shift_right)
                dve.drain()
                dve.tensor_copy(nb[:, :], nbi[:, :])
                dve.drain()
                dve.tensor_copy(cum[:, 0:1], nb[:, 0:1])
                for e in range(1, E):
                    dve.drain()
                    dve.tensor_tensor(cum[:, e:e + 1], cum[:, e - 1:e], nb[:, e:e + 1], ALU.add)
                dve.drain()
                dve.tensor_tensor(past[:, :, :], block_no[:, :].rearrange("p (b e) -> p b e", e=1).to_broadcast([P, NBLK, E]),
                                  cum[:, :].rearrange("p (b e) -> p b e", b=1).to_broadcast([P, NBLK, E]), ALU.is_ge)
                dve.drain()
                dve.tensor_reduce(eb[:, :], past[:, :, :], AX.X, ALU.add)
                dve.drain()
                dve.tensor_tensor(past[:, :, :], past[:, :, :],
                                  nb[:, :].rearrange("p (b e) -> p b e", b=1).to_broadcast([P, NBLK, E]), ALU.mult)
                dve.drain()
                dve.tensor_reduce(startb[:, :], past[:, :, :], AX.X, ALU.add)
                dve.drain()
                dve.tensor_tensor(rowf[:, :], block_no[:, :], startb[:, :], ALU.subtract)
                dve.drain()
                dve.tensor_scalar(startb[:, :], eb[:, :], float(REGION), None, ALU.mult)
                dve.drain()
                dve.scalar_tensor_tensor(out=rowf[:, :], in0=rowf[:, :], scalar=float(BLK), in1=startb[:, :],
                                         op0=ALU.mult, op1=ALU.add)
                dve.tensor_scalar(eb[:, :], eb[:, :], float(E - 1), None, ALU.min)
                dve.drain()
                dve.tensor_copy(row_i[:, :], rowf[:, :])
                dve.tensor_copy(exp_i[:, :], eb[:, :])
                dve.tensor_copy(base[:, :], region0[:, :])

            def block_mult(n, u):
                dve.wait_ge(s_block_silu, n + 1)
                at = 1536 * u + NC * BLK
                dve.scalar_tensor_tensor(out=eh32[u][:, :], in0=PSUM[:, at:at + NC * BLK], scalar=2.0 ** (SH - SX - SWT),
                                         in1=esil[u][:, :], op0=ALU.mult, op1=ALU.mult).then_inc(s_block_hidden, 1)

            def block_in(n, u, m):
                dve.wait_ge(s_block_turned, n + 1)
                dve.tensor_copy(eT[u][:, :, :], PE_T[:, 0:2 * BLK].rearrange("p (a t) -> p a t", a=2)).then_inc(s_block_T, 1)
                dve.tensor_scalar(second[:, u, :], xe[u][:, :, WORDS - 1], eb[:, bass.ds(m, 1)], float(T),
                                  ALU.not_equal, ALU.mult)
                dve.drain()
                dve.tensor_tensor(places[:, cols(m, HALVES)], second[:, u, :], xe[u][:, :, WORDS - 2], ALU.add).then_inc(s_block_places, 1)

            def block_low(n, u):
                dve.wait_ge(s_block_high, n + 1)
                low(ehT[u][:, 1, :, :], eh32[u][:, :].rearrange("p (c t) -> p c t", c=NC), ehT[u][:, 0, :, :], 0
                    ).then_inc(s_block_low, 1)

            def experts(f):
                n0, n1 = f * NBLK, (f + 1) * NBLK

                def step(n, u, ahead=True):
                    if ahead:
                        block_in(n + 1, 1 - u, n + 1 - n0)
                    block_low(n - 1, 1 - u)
                    block_mult(n, u)

                block_in(n0, 0, 0)
                block_in(n0 + 1, 1, 1)
                block_mult(n0, 0)
                block_in(n0 + 2, 0, 2)
                block_low(n0, 0)
                block_mult(n0 + 1, 1)
                with dve.Fori(0, (NBLK - 4) // 2) as i:
                    step(i * 2 + (n0 + 2), 0)
                    step(i * 2 + (n0 + 3), 1)
                step(n1 - 2, 0)
                step(n1 - 1, 1, ahead=False)
                block_low(n1 - 1, 1)

            def combine_first(g):
                dve.wait_ge(s_Y[g], 16 * K)
                xs = X3(g)
                for k in range(K):
                    for j in range(NJ):
                        dve.scalar_tensor_tensor(out=xs[:, j, :], in0=Y[g][:, k, j, :],
                                                 scalar=PR[:, cols(g, NJ * K, j * K + k, 1)], in1=xs[:, j, :],
                                                 op0=ALU.mult, op1=ALU.add)
                    last = dve.drain()
                last.then_inc(s_combined, 1)

            def combine_last(g, u):
                dve.wait_ge(s_YL[u], (g - u) * (16 * K // LAST) + 16 * K)
                xs = X3(g)
                for j in range(NJ):
                    dve.scalar_tensor_tensor(out=xs[:, j, :], in0=YL[u][:, 0, j, :], scalar=PR[:, cols(g, NJ * K, j * K, 1)],
                                             in1=xs[:, j, :], op0=ALU.mult, op1=ALU.add)
                dve.drain()
                dve.wait_ge(s_weighed, g + (NG - 1))
                dve.tensor_tensor(xs, xs, YL[u][:, 1, :, :], ALU.add).then_inc(s_combined, 1)

            def features(m, q):
                dve.wait_ge(s_qkv_parts, m * NJ + (2 * q + 2))
                dve.scalar_tensor_tensor(out=qk[:, q, :, :], in0=expo[:, q, :, :], scalar=1.0, in1=relu[:, q, :, :],
                                         op0=ALU.min, op1=ALU.add).then_inc(s_features, 1)

            def attend(m, q, a):
                j = 2 * q + a
                dve.wait_ge(s_running_sums, m * NJ + (j + 1))
                q4 = qk[:, q, a, 0:D].rearrange("p (h i j) -> p h i j", h=HEADS, j=1).to_broadcast([P, HEADS, HD, VD])
                dve.tensor_tensor(prod[:, a, :].rearrange("p (h i j) -> p h i j", h=HEADS, i=HD),
                                  PKV[:, :].rearrange("p (h i j) -> p h i j", h=HEADS, i=HD), q4, ALU.mult).then_inc(s_sums_read, 1)
                dve.drain()
                dve.tensor_reduce(num[:, j, :, :], prod[:, a, :].rearrange("p (h i j) -> p h j i", h=HEADS, i=HD),
                                  AX.X, ALU.add)

            def divide(m):
                dve.drain()
                dve.tensor_scalar(rden[:, :, :], num[:, :, :, HD], EPS_DEN, None, ALU.add)
                dve.drain()
                dve.reciprocal(rden[:, :, :], rden[:, :, :])
                dve.drain()
                dve.tensor_tensor(y32[:, :, :].rearrange("p j (h i) -> p j h i", h=HEADS), num[:, :, :, 0:HD],
                                  rden[:, :, :].rearrange("p j (h i) -> p j h i", i=1).to_broadcast([P, NJ, HEADS, HD]),
                                  ALU.mult).then_inc(s_y, 1)

            def y_low(m):
                dve.wait_ge(s_y_high, m + 1)
                low(ya[:, 1, :, :], y32[:, :, :], ya[:, 0, :, :], SY).then_inc(s_y_low, 1)

            def attention_add(m):
                dve.wait_ge(s_projected, m + 1)
                xg = X[:, cols(m, GT)]
                dve.scalar_tensor_tensor(out=xg, in0=PO[:, :], scalar=2.0 ** -(SY + SWT), in1=xg, op0=ALU.mult,
                                         op1=ALU.add).then_inc(s_attention_added, 1)
                dve.drain()

            dve.wait_ge(s_first_tokens, 32)

            def row_low(n, u):
                dve.wait_ge(s_norm_high, n + 1)
                dve.tensor_tensor(row[u][:, :, D // 2:D].bitcast(F16), xn[:, slot(n, u), :, :],
                                  row[u][:, :, 0:D // 2].bitcast(F16), ALU.subtract).then_inc(s_norm_low, 1)

            def first_ffn(n, u):
                edge = isinstance(n, int)
                ahead = not (edge and n == NG - 1)
                choose(n, u, n)
                if not (edge and n == 0):
                    shared_low(n - 1)
                place(n, u, n)
                if not ahead:
                    ends()
                for h in range(2):
                    shared(n, 0, h)
                probabilities(n, n)
                if ahead:
                    row_low(n + 1, 1 - u)
                for h in range(2):
                    shared(n, 1, h)
                if not (edge and n == 0):
                    shared_add(n - 1, n - 1)
                if edge and n == 0:
                    dve.wait_ge(s_tokens, 16 * (NG - 2))
                    moments(0, 2)
                    moments(1, 3)
                if u == 0 and not (edge and n == NG - 2):
                    deviations(2)
                if u == 1 and not (edge and n >= NG - 3):
                    moments(0, n + 3)
                    moments(1, n + 4)
                if edge and n < 2:
                    expert_weights(n)
                if edge and n == NG - 2:
                    expert_weights(2)

            ffn[0] = 0
            moments(0, 0)
            moments(1, 1)
            deviations(2)
            dve.wait_ge(s_constants, 1)
            dve.wait_ge(s_weights_high, 1)
            o = 0
            for w, n in ((GW, E), (SGW, FS), (SUW, FS), (AW, 3 * D), (PW, D)):
                low(w[:, 1, :], small_w[:, o:o + n], w[:, 0, :], SWT)
                o += n
            low(SDW[0:SW, 1, :], small_w[0:SW, o:o + SC * D], SDW[0:SW, 0, :], SWT)
            low(bias_l[:, :], bias_f[:, :], bias[:, :], SBIAS)
            dve.drain()
            dve.tensor_scalar(bias_l[:, :], bias_l[:, :], is_row[:, 1:2], None, ALU.mult)
            dve.drain()
            dve.scalar_tensor_tensor(out=bias[:, :], in0=bias[:, :], scalar=is_row[:, 0:1], in1=bias_l[:, :],
                                     op0=ALU.mult, op1=ALU.add)
            dve.drain().then_inc(s_weights_low, 1)

            dve.tensor_copy(base[:, :], region0[:, :])
            row_low(0, 0)
            pairs(dve, 0, NG, first_ffn, tail=4)
            shared_low(NG - 1)
            tables()
            shared_add(NG - 1, NG - 1)
            phase_end(dve, 1)
            experts(0)
            phase_end(dve, 2)

            def streams(m, u, route, attending, ready, settle):
                n = m + NG
                if route:
                    moments(0, m)
                if route or ready:
                    deviations(1)
                if isinstance(m, int) and m == -2:
                    combine_first(1)
                if attending:
                    attend(m + 1, 0, 1)
                end = isinstance(m, int) and m == NG
                if settle:
                    place(n - 1, 1 - u, m - 1)
                    if end:
                        ends()
                    for h in range(2):
                        shared(n - 1, 0, h)
                    probabilities(n - 1, m - 1)
                if attending:
                    attend(m + 1, 1, 0)
                if settle:
                    for h in range(2):
                        shared(n - 1, 1, h)
                if route:
                    choose(n, u, m)
                if settle:
                    shared_low(n - 1)
                    if end:
                        tables()
                if attending:
                    attend(m + 1, 1, 1)
                    divide(m + 1)
                if ready:
                    features(m + 2, 0)
                if attending:
                    y_low(m + 1)
                if ready:
                    features(m + 2, 1)
                if settle:
                    shared_add(n - 1, m - 1)
                if ready and not (isinstance(m, int) and m == NG - 3):
                    dve.wait_ge(s_combined, m + 4)
                    moments(1, m + 3)
                if ready:
                    attend(m + 2, 0, 0)
                if attending:
                    attention_add(m + 1)

            ffn[0] = 1
            for u in range(2):
                dve.tensor_scalar(row[u][:, :, WORDS - 2], row[u][:, :, WORDS - 2], float(-T), None, ALU.add)
            combine_first(0)
            moments(1, 0)
            streams_of(dve, streams)
            phase_end(dve, 3)
            experts(1)
            phase_end(dve, 4)
            with dve.Fori(0, NG // LAST) as i:
                for u in range(LAST):
                    combine_last(i * LAST + u, u)


_INS = ['L0_attn_x', 'L0_attn_W_attn', 'L0_attn_b_attn', 'L0_attn_W_proj', 'L0_attn_b_proj', 'L0_ffn_gate_w',
        'L0_ffn_Wg', 'L0_ffn_Wu', 'L0_ffn_Wd', 'L0_ffn_Sg', 'L0_ffn_Su', 'L0_ffn_Sd']


def kernel(**inputs):
    import numpy as _np
    import concourse.bacc as _bacc
    from concourse import mybir as _mybir
    from concourse.bass_utils import run_bass_kernel_spmd as _run

    nc = _bacc.Bacc("TRN2", target_bir_lowering=False, num_devices=1)
    arrays, args = {}, []
    for name in _INS:
        a = _np.ascontiguousarray(inputs[name])
        if name == 'L0_attn_x':
            a = a.reshape(T, D)
        arrays[f"in_{name}_dram"] = a
        args.append(nc.dram_tensor(f"in_{name}_dram", a.shape, _mybir.dt.from_np(a.dtype), kind="ExternalInput").ap())
    args.append(nc.dram_tensor("out_0_dram", (T, D), _mybir.dt.float32, kind="ExternalOutput").ap())
    macaron(nc, *args)
    r = _run(nc, [arrays], core_ids=[0])
    return r.results[0]["out_0_dram"].reshape(B, S, D)
```
